# Optimizing a Trainium2 kernel written in Bass

```python
import numpy as np
import jax
import jax.numpy as jnp

def _softmax(x, axis=-1):
    return jax.nn.softmax(x, axis=axis)

def _gelu(x):
    return jax.nn.gelu(x, approximate=True)

def _silu(x):
    return jax.nn.silu(x)

def _sigmoid(x):
    return jax.nn.sigmoid(x)

def _layernorm(x, axis=-1, eps=1e-05):
    m = jnp.mean(x, axis=axis, keepdims=True)
    v = jnp.var(x, axis=axis, keepdims=True)
    return (x - m) / jnp.sqrt(v + eps)

def _scatter_add(tgt, idx, src, axis=0):
    return tgt.at[idx].add(src)

def _segment_sum(src, seg, n):
    return jax.ops.segment_sum(src, seg, n)
kernel_name = 'mk_decoder_preln_d2_seqx_r4_122df2'

def setup_inputs(seed: int=0):
    np.random.seed(seed)
    _w = jnp.asarray

    def _rec_inputs():
        import jax
        import jax.numpy as jnp
        _rk = jax.random.key(seed)
        x = -0.000125 + 0.9999 * jax.random.normal(jax.random.fold_in(_rk, 1), (4, 512, 512), jnp.float32)
        _lenS = 512 - jax.random.randint(jax.random.fold_in(_rk, 7), (4,), 0, max(1, 512 // 4) + 1, jnp.int32)
        _lenS2 = 512 - jax.random.randint(jax.random.fold_in(_rk, 8), (4,), 0, max(1, 512 // 4) + 1, jnp.int32)
        fside_BxS2xS2_0 = -3.05549e-07 + 0.0199987 * jax.random.normal(jax.random.fold_in(_rk, 11), (4, 512, 512), jnp.float32)
        _ctx_1024P = jax.random.normal(jax.random.fold_in(_rk, 12), (4, 16, 256), jnp.float32)
        _ctx_1024c = jax.random.dirichlet(jax.random.fold_in(_rk, 512), 0.3 * jnp.ones((16,), jnp.float32), (4, 512))
        _ctx_1024t = jnp.einsum('bsk,bkd->bsd', _ctx_1024c, _ctx_1024P)
        _ctx_1024t = _ctx_1024t * jax.lax.rsqrt(jnp.mean(jnp.square(_ctx_1024t)) + 1e-12) * 0.953939
        ctx_1024 = 6.82029e-06 + 0.0200006 * (_ctx_1024t + 0.3 * jax.random.normal(jax.random.fold_in(_rk, 612), (4, 512, 256), jnp.float32))
        fside_BxSx2_0 = jax.random.uniform(jax.random.fold_in(_rk, 13), (4, 512, 2), jnp.float32, 0.0, 0.999707)
        return (x, fside_BxS2xS2_0, ctx_1024, fside_BxSx2_0)
    x, fside_BxS2xS2_0, ctx_1024, fside_BxSx2_0 = _rec_inputs()

    def _L0_attn_setup():
        import jax, jax.numpy as jnp
        from jax import lax
        import numpy as np
        D_MODEL, D_STATE, D_CONV, DT_RANK = (512, 16, 4, 128)
        B, L = (2, 256)
        key = jax.random.key(seed)
        ks = jax.random.split(key, 6)
        return {'x': jax.random.normal(ks[0], (B, L, D_MODEL), dtype=jnp.float32), 'conv_w': jax.random.normal(ks[1], (D_MODEL, 1, D_CONV), dtype=jnp.float32) * 0.2, 'conv_b': jnp.zeros((D_MODEL,), dtype=jnp.float32), 'xproj_w': jax.random.normal(ks[2], (DT_RANK + 2 * D_STATE, D_MODEL), dtype=jnp.float32) * 0.02, 'dtproj_w': jax.random.normal(ks[3], (D_MODEL, DT_RANK), dtype=jnp.float32) * 0.05, 'dtproj_b': jnp.zeros((D_MODEL,), dtype=jnp.float32), 'A_log': jnp.zeros((D_MODEL, D_STATE), dtype=jnp.float32), 'D_skip': jnp.ones((D_MODEL,), dtype=jnp.float32)}
    _L0_attn_all = _L0_attn_setup()
    _L0_attn_in = {k: v for k, v in _L0_attn_all.items() if k in ('conv_w', 'conv_b', 'xproj_w', 'dtproj_w', 'dtproj_b', 'A_log', 'D_skip')}
    del _L0_attn_all

    def _L0_xattn_setup():
        import jax, jax.numpy as jnp
        import numpy as np
        EPS = 1e-06
        QMAX = 127.0

        def _smooth_quant_linear(x, w):
            amax_x = jnp.max(jnp.abs(x), axis=0)
            amax_w = jnp.max(jnp.abs(w), axis=0)
            s = jnp.sqrt(jnp.maximum(amax_x, EPS) / jnp.maximum(amax_w, EPS))
            s = jnp.maximum(s, EPS)
            xs = x / s
            ws = w * s
            x_scale = jnp.maximum(jnp.max(jnp.abs(xs), axis=-1, keepdims=True), EPS) / QMAX
            w_scale = jnp.maximum(jnp.max(jnp.abs(ws), axis=-1, keepdims=True), EPS) / QMAX
            x_q = jnp.clip(jnp.round(xs / x_scale), -QMAX, QMAX)
            w_q = jnp.clip(jnp.round(ws / w_scale), -QMAX, QMAX)
            return x_q @ w_q.T * x_scale * w_scale.T

        def _expert_forward(xe, guw, dw):
            h = _smooth_quant_linear(xe, guw)
            gate, up = jnp.split(h, 2, axis=-1)
            a = jax.nn.silu(gate) * up
            return _smooth_quant_linear(a, dw)
        key = jax.random.key(seed)
        k1, k2, k3 = jax.random.split(key, 3)
        E, T, D, I = (8, 512, 512, 256)
        x = jax.random.normal(k1, (E, T, D), dtype=jnp.float32)
        gate_up_weight = jax.random.normal(k2, (E, 2 * I, D), dtype=jnp.float32) * 0.02
        down_weight = jax.random.normal(k3, (E, D, I), dtype=jnp.float32) * 0.02
        return {'x': x, 'gate_up_weight': gate_up_weight, 'down_weight': down_weight}
    _L0_xattn_all = _L0_xattn_setup()
    _L0_xattn_in = {k: v for k, v in _L0_xattn_all.items() if k in ()}
    del _L0_xattn_all

    def _L0_ffn_setup():
        import jax, jax.numpy as jnp
        import numpy as np
        E = 8
        TOP_K = 2
        D = 512
        DE = 352
        DS = 704
        B, S = (2, 512)
        key = jax.random.key(seed)
        ks = jax.random.split(key, 8)
        std = 0.02
        return {'x': jax.random.normal(ks[0], (B, S, D), jnp.float32), 'W_router': jax.random.normal(ks[1], (D, E), jnp.float32) * std, 'We_gate': jax.random.normal(ks[2], (E, D, DE), jnp.float32) * std, 'We_up': jax.random.normal(ks[3], (E, D, DE), jnp.float32) * std, 'We_down': jax.random.normal(ks[4], (E, DE, D), jnp.float32) * std, 'Ws_gate': jax.random.normal(ks[5], (D, DS), jnp.float32) * std, 'Ws_up': jax.random.normal(ks[6], (D, DS), jnp.float32) * std, 'Ws_down': jax.random.normal(ks[7], (DS, D), jnp.float32) * std}
    _L0_ffn_all = _L0_ffn_setup()
    _L0_ffn_in = {k: v for k, v in _L0_ffn_all.items() if k in ('W_router', 'We_gate', 'We_up', 'We_down', 'Ws_gate', 'Ws_up', 'Ws_down')}
    del _L0_ffn_all

    def _L1_attn_setup():
        import jax, jax.numpy as jnp
        import numpy as np
        from jax import lax
        B, T = (2, 512)
        HID = 512
        H, K, KC = (16, 128, 4)
        D = H * K
        EPS = 1e-05
        SCALE = K ** (-0.5)

        def causal_conv_silu(x, w, b):
            xp = jnp.pad(jnp.swapaxes(x, 1, 2), ((0, 0), (0, 0), (KC - 1, 0)))
            y = lax.conv_general_dilated(xp, w[:, None, :], (1,), 'VALID', feature_group_count=D)
            return jax.nn.silu(jnp.swapaxes(y, 1, 2) + b)

        def l2norm(x):
            return x * lax.rsqrt(jnp.sum(x * x, -1, keepdims=True) + 1e-06)

        def kda_scan(q, k, v, g, beta):
            qT, kT, vT, gT, bT = (jnp.moveaxis(a, 1, 0) for a in (q, k, v, g, beta))
            S0 = jnp.zeros((q.shape[0], H, K, K), q.dtype)

            def step(S, inp):
                qt, kt, vt, gt, bt = inp
                S = S * jnp.exp(gt)[..., None]
                vd = (vt - jnp.einsum('bhkv,bhk->bhv', S, kt)) * bt[..., None]
                S = S + kt[..., None] * vd[:, :, None, :]
                return (S, jnp.einsum('bhkv,bhk->bhv', S, qt))
            _, o = lax.scan(step, S0, (qT, kT, vT, gT, bT))
            return jnp.moveaxis(o, 0, 1)

        def _forward(x, Wq, Wk, Wv, conv_q_w, conv_q_b, conv_k_w, conv_k_b, conv_v_w, conv_v_b, Wfa, Wfb, A_log, dt_bias, Wb, Wga, Wgb, o_norm_w, Wo):
            b, t = x.shape[:2]
            q = causal_conv_silu(x @ Wq, conv_q_w, conv_q_b).reshape(b, t, H, K)
            k = causal_conv_silu(x @ Wk, conv_k_w, conv_k_b).reshape(b, t, H, K)
            v = causal_conv_silu(x @ Wv, conv_v_w, conv_v_b).reshape(b, t, H, K)
            g = jax.nn.softplus(x @ Wfa @ Wfb + dt_bias).reshape(b, t, H, K)
            g = -jnp.exp(A_log)[None, None, :, None] * g
            beta = jax.nn.sigmoid(x @ Wb)
            q = l2norm(q) * SCALE
            k = l2norm(k)
            o = kda_scan(q, k, v, g, beta)
            gate = (x @ Wga @ Wgb).reshape(b, t, H, K)
            var = jnp.mean(o * o, -1, keepdims=True)
            o = o * lax.rsqrt(var + EPS) * o_norm_w * jax.nn.sigmoid(gate)
            return o.reshape(b, t, D) @ Wo
        key = jax.random.key(seed)
        ks = jax.random.split(key, 16)
        s = 0.02
        f32 = jnp.float32
        return {'x': jax.random.normal(ks[0], (B, T, HID), f32), 'Wq': jax.random.normal(ks[1], (HID, D), f32) * s, 'Wk': jax.random.normal(ks[2], (HID, D), f32) * s, 'Wv': jax.random.normal(ks[3], (HID, D), f32) * s, 'conv_q_w': jax.random.normal(ks[4], (D, KC), f32) * 0.2, 'conv_q_b': jnp.zeros((D,), f32), 'conv_k_w': jax.random.normal(ks[5], (D, KC), f32) * 0.2, 'conv_k_b': jnp.zeros((D,), f32), 'conv_v_w': jax.random.normal(ks[6], (D, KC), f32) * 0.2, 'conv_v_b': jnp.zeros((D,), f32), 'Wfa': jax.random.normal(ks[7], (HID, K), f32) * s, 'Wfb': jax.random.normal(ks[8], (K, D), f32) * s, 'A_log': jnp.log(jax.random.uniform(ks[9], (H,), f32, 1.0, 16.0)), 'dt_bias': jnp.zeros((D,), f32), 'Wb': jax.random.normal(ks[10], (HID, H), f32) * s, 'Wga': jax.random.normal(ks[11], (HID, K), f32) * s, 'Wgb': jax.random.normal(ks[12], (K, D), f32) * s, 'o_norm_w': jnp.ones((K,), f32), 'Wo': jax.random.normal(ks[13], (D, HID), f32) * s}
    _L1_attn_all = _L1_attn_setup()
    _L1_attn_in = {k: v for k, v in _L1_attn_all.items() if k in ('Wq', 'Wk', 'Wv', 'conv_q_w', 'conv_q_b', 'conv_k_w', 'conv_k_b', 'conv_v_w', 'conv_v_b', 'Wfa', 'Wfb', 'A_log', 'dt_bias', 'Wb', 'Wga', 'Wgb', 'o_norm_w', 'Wo')}
    del _L1_attn_all

    def _L1_xattn_setup():
        import jax, jax.numpy as jnp
        import numpy as np
        DIM = 512
        CTX_DIM = 256
        N_HEADS = 32
        HEAD_DIM = DIM // N_HEADS
        POS_DIM = 2
        B, N, CTXN = (2, 512, 512)
        ROPE_BASE = 10000.0

        def apply_axial_rope(x, pos):
            b, n, h, d = x.shape
            p = pos.shape[-1]
            dpa = d // p
            half = dpa // 2
            freqs = ROPE_BASE ** (-jnp.arange(half, dtype=x.dtype) / half)
            ang = pos[..., :, None] * freqs
            cos = jnp.cos(ang)[:, :, None, :, :]
            sin = jnp.sin(ang)[:, :, None, :, :]
            xr = x.reshape(b, n, h, p, half, 2)
            x1, x2 = (xr[..., 0], xr[..., 1])
            out = jnp.stack([x1 * cos - x2 * sin, x1 * sin + x2 * cos], axis=-1)
            return out.reshape(b, n, h, d)
        key = jax.random.key(seed)
        ks = jax.random.split(key, 8)
        x = jax.random.normal(ks[0], (B, N, DIM), jnp.float32)
        ctx = jax.random.normal(ks[1], (B, CTXN, CTX_DIM), jnp.float32)
        pos_map = jax.random.uniform(ks[2], (B, N, POS_DIM), jnp.float32)
        ctx_pos_map = jax.random.uniform(ks[3], (B, CTXN, POS_DIM), jnp.float32)
        Wq = jax.random.normal(ks[4], (DIM, DIM), jnp.float32) / np.sqrt(DIM)
        Wkv = jax.random.normal(ks[5], (CTX_DIM, 2 * DIM), jnp.float32) / np.sqrt(CTX_DIM)
        Wout = jax.random.normal(ks[6], (DIM, DIM), jnp.float32) / np.sqrt(DIM)
        bout = jnp.zeros((DIM,), jnp.float32)
        return {'x': x, 'ctx': ctx, 'pos_map': pos_map, 'ctx_pos_map': ctx_pos_map, 'Wq': Wq, 'Wkv': Wkv, 'Wout': Wout, 'bout': bout}
    _L1_xattn_all = _L1_xattn_setup()
    _L1_xattn_in = {k: v for k, v in _L1_xattn_all.items() if k in ('Wq', 'Wkv', 'Wout', 'bout')}
    del _L1_xattn_all

    def _L1_ffn_setup():
        import jax, jax.numpy as jnp
        import numpy as np
        D_MODEL = 512
        HIDDEN = 1408
        BATCH, SEQ = (4, 512)

        def _activation_quant(x):
            scale = 127.0 / jnp.clip(jnp.max(jnp.abs(x), axis=-1, keepdims=True), 1e-05, None)
            xq = jnp.clip(jnp.round(x * scale), -128.0, 127.0) / scale
            return x + jax.lax.stop_gradient(xq - x)

        def _weight_quant(w):
            scale = 1.0 / jnp.clip(jnp.mean(jnp.abs(w)), 1e-05, None)
            wq = jnp.clip(jnp.round(w * scale), -1.0, 1.0) / scale
            return w + jax.lax.stop_gradient(wq - w)

        def _bitlinear(x, w):
            return jnp.einsum('bsi,oi->bso', _activation_quant(x), _weight_quant(w))
        key = jax.random.key(seed)
        kx, k1, k2, k3 = jax.random.split(key, 4)
        x = jax.random.normal(kx, (BATCH, SEQ, D_MODEL), dtype=jnp.float32)
        w1 = jax.random.normal(k1, (HIDDEN, D_MODEL), dtype=jnp.float32) * 0.02
        w2 = jax.random.normal(k2, (HIDDEN, D_MODEL), dtype=jnp.float32) * 0.02
        w3 = jax.random.normal(k3, (D_MODEL, HIDDEN), dtype=jnp.float32) * 0.02
        return {'x': x, 'w1': w1, 'w2': w2, 'w3': w3}
    _L1_ffn_all = _L1_ffn_setup()
    _L1_ffn_in = {k: v for k, v in _L1_ffn_all.items() if k in ('w1', 'w2', 'w3')}
    del _L1_ffn_all
    return {'x': x, 'fside_BxS2xS2_0': fside_BxS2xS2_0, 'ctx_1024': ctx_1024, 'fside_BxSx2_0': fside_BxSx2_0, 'L0_attn_conv_w': _L0_attn_in['conv_w'], 'L0_attn_conv_b': _L0_attn_in['conv_b'], 'L0_attn_xproj_w': _L0_attn_in['xproj_w'], 'L0_attn_dtproj_w': _L0_attn_in['dtproj_w'], 'L0_attn_dtproj_b': _L0_attn_in['dtproj_b'], 'L0_attn_A_log': _L0_attn_in['A_log'], 'L0_attn_D_skip': _L0_attn_in['D_skip'], 'L0_ffn_W_router': _L0_ffn_in['W_router'], 'L0_ffn_We_gate': _L0_ffn_in['We_gate'], 'L0_ffn_We_up': _L0_ffn_in['We_up'], 'L0_ffn_We_down': _L0_ffn_in['We_down'], 'L0_ffn_Ws_gate': _L0_ffn_in['Ws_gate'], 'L0_ffn_Ws_up': _L0_ffn_in['Ws_up'], 'L0_ffn_Ws_down': _L0_ffn_in['Ws_down'], 'L1_attn_Wq': _L1_attn_in['Wq'], 'L1_attn_Wk': _L1_attn_in['Wk'], 'L1_attn_Wv': _L1_attn_in['Wv'], 'L1_attn_conv_q_w': _L1_attn_in['conv_q_w'], 'L1_attn_conv_q_b': _L1_attn_in['conv_q_b'], 'L1_attn_conv_k_w': _L1_attn_in['conv_k_w'], 'L1_attn_conv_k_b': _L1_attn_in['conv_k_b'], 'L1_attn_conv_v_w': _L1_attn_in['conv_v_w'], 'L1_attn_conv_v_b': _L1_attn_in['conv_v_b'], 'L1_attn_Wfa': _L1_attn_in['Wfa'], 'L1_attn_Wfb': _L1_attn_in['Wfb'], 'L1_attn_A_log': _L1_attn_in['A_log'], 'L1_attn_dt_bias': _L1_attn_in['dt_bias'], 'L1_attn_Wb': _L1_attn_in['Wb'], 'L1_attn_Wga': _L1_attn_in['Wga'], 'L1_attn_Wgb': _L1_attn_in['Wgb'], 'L1_attn_o_norm_w': _L1_attn_in['o_norm_w'], 'L1_attn_Wo': _L1_attn_in['Wo'], 'L1_xattn_Wq': _L1_xattn_in['Wq'], 'L1_xattn_Wkv': _L1_xattn_in['Wkv'], 'L1_xattn_Wout': _L1_xattn_in['Wout'], 'L1_xattn_bout': _L1_xattn_in['bout'], 'L1_ffn_w1': _L1_ffn_in['w1'], 'L1_ffn_w2': _L1_ffn_in['w2'], 'L1_ffn_w3': _L1_ffn_in['w3']}

def reference(x, fside_BxS2xS2_0, ctx_1024, fside_BxSx2_0, L0_attn_conv_w, L0_attn_conv_b, L0_attn_xproj_w, L0_attn_dtproj_w, L0_attn_dtproj_b, L0_attn_A_log, L0_attn_D_skip, L0_ffn_W_router, L0_ffn_We_gate, L0_ffn_We_up, L0_ffn_We_down, L0_ffn_Ws_gate, L0_ffn_Ws_up, L0_ffn_Ws_down, L1_attn_Wq, L1_attn_Wk, L1_attn_Wv, L1_attn_conv_q_w, L1_attn_conv_q_b, L1_attn_conv_k_w, L1_attn_conv_k_b, L1_attn_conv_v_w, L1_attn_conv_v_b, L1_attn_Wfa, L1_attn_Wfb, L1_attn_A_log, L1_attn_dt_bias, L1_attn_Wb, L1_attn_Wga, L1_attn_Wgb, L1_attn_o_norm_w, L1_attn_Wo, L1_xattn_Wq, L1_xattn_Wkv, L1_xattn_Wout, L1_xattn_bout, L1_ffn_w1, L1_ffn_w2, L1_ffn_w3):
    import jax
    import jax.numpy as jnp

    def _L0_attn_ref(x, conv_w, conv_b, xproj_w, dtproj_w, dtproj_b, A_log, D_skip):
        import jax, jax.numpy as jnp
        from jax import lax
        import numpy as np
        D_MODEL, D_STATE, D_CONV, DT_RANK = (512, 16, 4, 128)
        B, L = (2, 256)
        b, l, d = x.shape
        k = conv_w.shape[-1]
        n = A_log.shape[-1]
        r = dtproj_w.shape[-1]
        xt = jnp.transpose(x, (0, 2, 1))
        xp = jnp.pad(xt, ((0, 0), (0, 0), (k - 1, 0)))
        u = lax.conv_general_dilated(xp, conv_w, window_strides=(1,), padding='VALID', feature_group_count=d) + conv_b[None, :, None]
        u_bld = jnp.transpose(u, (0, 2, 1))
        x_dbl = jnp.einsum('bld,ed->ble', u_bld, xproj_w)
        dt = x_dbl[..., :r]
        Bm = x_dbl[..., r:r + n]
        Cm = x_dbl[..., r + n:]
        delta = jax.nn.softplus(jnp.einsum('blr,dr->bld', dt, dtproj_w) + dtproj_b)
        A = -jnp.exp(A_log)
        deltaA = jnp.exp(delta[..., None] * A)
        deltaBu = delta[..., None] * Bm[:, :, None, :] * u_bld[..., None]

        def step(h, inp):
            dA, dBu, c = inp
            h = dA * h + dBu
            y = jnp.einsum('bdn,bn->bd', h, c)
            return (h, y)
        h0 = jnp.zeros((b, d, n), dtype=x.dtype)
        _, ys = lax.scan(step, h0, (jnp.transpose(deltaA, (1, 0, 2, 3)), jnp.transpose(deltaBu, (1, 0, 2, 3)), jnp.transpose(Cm, (1, 0, 2))))
        y = jnp.transpose(ys, (1, 0, 2)) + u_bld * D_skip
        return y

    def _L0_xattn_ref(x, gate_up_weight, down_weight):
        import jax, jax.numpy as jnp
        import numpy as np
        EPS = 1e-06
        QMAX = 127.0

        def _smooth_quant_linear(x, w):
            amax_x = jnp.max(jnp.abs(x), axis=0)
            amax_w = jnp.max(jnp.abs(w), axis=0)
            s = jnp.sqrt(jnp.maximum(amax_x, EPS) / jnp.maximum(amax_w, EPS))
            s = jnp.maximum(s, EPS)
            xs = x / s
            ws = w * s
            x_scale = jnp.maximum(jnp.max(jnp.abs(xs), axis=-1, keepdims=True), EPS) / QMAX
            w_scale = jnp.maximum(jnp.max(jnp.abs(ws), axis=-1, keepdims=True), EPS) / QMAX
            x_q = jnp.clip(jnp.round(xs / x_scale), -QMAX, QMAX)
            w_q = jnp.clip(jnp.round(ws / w_scale), -QMAX, QMAX)
            return x_q @ w_q.T * x_scale * w_scale.T

        def _expert_forward(xe, guw, dw):
            h = _smooth_quant_linear(xe, guw)
            gate, up = jnp.split(h, 2, axis=-1)
            a = jax.nn.silu(gate) * up
            return _smooth_quant_linear(a, dw)
        return jax.vmap(_expert_forward)(x, gate_up_weight, down_weight)

    def _L0_ffn_ref(x, W_router, We_gate, We_up, We_down, Ws_gate, Ws_up, Ws_down):
        import jax, jax.numpy as jnp
        import numpy as np
        E = 8
        TOP_K = 2
        D = 512
        DE = 352
        DS = 704
        B, S = (2, 512)
        b, s, d = x.shape
        shared = jax.nn.silu(x @ Ws_gate) * (x @ Ws_up) @ Ws_down
        scores = jax.nn.softmax(x @ W_router, axis=-1)
        topk_vals, topk_idx = jax.lax.top_k(scores, TOP_K)
        onehot = jax.nn.one_hot(topk_idx, E, dtype=x.dtype)
        combine = jnp.einsum('bsk,bske->bse', topk_vals, onehot)
        combine = combine.reshape(b * s, E)
        xf = x.reshape(b * s, d)
        h = jax.nn.silu(jnp.einsum('td,edh->eth', xf, We_gate)) * jnp.einsum('td,edh->eth', xf, We_up)
        y_all = jnp.einsum('eth,ehd->etd', h, We_down)
        routed = jnp.einsum('etd,te->td', y_all, combine)
        return routed.reshape(b, s, d) + shared

    def _L1_attn_ref(x, Wq, Wk, Wv, conv_q_w, conv_q_b, conv_k_w, conv_k_b, conv_v_w, conv_v_b, Wfa, Wfb, A_log, dt_bias, Wb, Wga, Wgb, o_norm_w, Wo):
        import jax, jax.numpy as jnp
        import numpy as np
        from jax import lax
        B, T = (2, 512)
        HID = 512
        H, K, KC = (16, 128, 4)
        D = H * K
        EPS = 1e-05
        SCALE = K ** (-0.5)

        def causal_conv_silu(x, w, b):
            xp = jnp.pad(jnp.swapaxes(x, 1, 2), ((0, 0), (0, 0), (KC - 1, 0)))
            y = lax.conv_general_dilated(xp, w[:, None, :], (1,), 'VALID', feature_group_count=D)
            return jax.nn.silu(jnp.swapaxes(y, 1, 2) + b)

        def l2norm(x):
            return x * lax.rsqrt(jnp.sum(x * x, -1, keepdims=True) + 1e-06)

        def kda_scan(q, k, v, g, beta):
            qT, kT, vT, gT, bT = (jnp.moveaxis(a, 1, 0) for a in (q, k, v, g, beta))
            S0 = jnp.zeros((q.shape[0], H, K, K), q.dtype)

            def step(S, inp):
                qt, kt, vt, gt, bt = inp
                S = S * jnp.exp(gt)[..., None]
                vd = (vt - jnp.einsum('bhkv,bhk->bhv', S, kt)) * bt[..., None]
                S = S + kt[..., None] * vd[:, :, None, :]
                return (S, jnp.einsum('bhkv,bhk->bhv', S, qt))
            _, o = lax.scan(step, S0, (qT, kT, vT, gT, bT))
            return jnp.moveaxis(o, 0, 1)

        def _forward(x, Wq, Wk, Wv, conv_q_w, conv_q_b, conv_k_w, conv_k_b, conv_v_w, conv_v_b, Wfa, Wfb, A_log, dt_bias, Wb, Wga, Wgb, o_norm_w, Wo):
            b, t = x.shape[:2]
            q = causal_conv_silu(x @ Wq, conv_q_w, conv_q_b).reshape(b, t, H, K)
            k = causal_conv_silu(x @ Wk, conv_k_w, conv_k_b).reshape(b, t, H, K)
            v = causal_conv_silu(x @ Wv, conv_v_w, conv_v_b).reshape(b, t, H, K)
            g = jax.nn.softplus(x @ Wfa @ Wfb + dt_bias).reshape(b, t, H, K)
            g = -jnp.exp(A_log)[None, None, :, None] * g
            beta = jax.nn.sigmoid(x @ Wb)
            q = l2norm(q) * SCALE
            k = l2norm(k)
            o = kda_scan(q, k, v, g, beta)
            gate = (x @ Wga @ Wgb).reshape(b, t, H, K)
            var = jnp.mean(o * o, -1, keepdims=True)
            o = o * lax.rsqrt(var + EPS) * o_norm_w * jax.nn.sigmoid(gate)
            return o.reshape(b, t, D) @ Wo
        return _forward(x, Wq, Wk, Wv, conv_q_w, conv_q_b, conv_k_w, conv_k_b, conv_v_w, conv_v_b, Wfa, Wfb, A_log, dt_bias, Wb, Wga, Wgb, o_norm_w, Wo)

    def _L1_xattn_ref(x, ctx, pos_map, ctx_pos_map, Wq, Wkv, Wout, bout):
        import jax, jax.numpy as jnp
        import numpy as np
        DIM = 512
        CTX_DIM = 256
        N_HEADS = 32
        HEAD_DIM = DIM // N_HEADS
        POS_DIM = 2
        B, N, CTXN = (2, 512, 512)
        ROPE_BASE = 10000.0

        def apply_axial_rope(x, pos):
            b, n, h, d = x.shape
            p = pos.shape[-1]
            dpa = d // p
            half = dpa // 2
            freqs = ROPE_BASE ** (-jnp.arange(half, dtype=x.dtype) / half)
            ang = pos[..., :, None] * freqs
            cos = jnp.cos(ang)[:, :, None, :, :]
            sin = jnp.sin(ang)[:, :, None, :, :]
            xr = x.reshape(b, n, h, p, half, 2)
            x1, x2 = (xr[..., 0], xr[..., 1])
            out = jnp.stack([x1 * cos - x2 * sin, x1 * sin + x2 * cos], axis=-1)
            return out.reshape(b, n, h, d)
        b, n, _ = x.shape
        ctx_n = ctx.shape[1]
        q = (x @ Wq).reshape(b, n, N_HEADS, HEAD_DIM)
        k, v = jnp.split(ctx @ Wkv, 2, axis=-1)
        k = k.reshape(b, ctx_n, N_HEADS, HEAD_DIM)
        v = v.reshape(b, ctx_n, N_HEADS, HEAD_DIM)
        q = apply_axial_rope(q, pos_map)
        k = apply_axial_rope(k, ctx_pos_map)
        scale = 1.0 / np.sqrt(HEAD_DIM).astype(np.float32)
        logits = jnp.einsum('bqhd,bkhd->bhqk', q, k) * scale
        w = jax.nn.softmax(logits, axis=-1)
        attn = jnp.einsum('bhqk,bkhd->bqhd', w, v)
        attn = attn.reshape(b, n, N_HEADS * HEAD_DIM)
        return attn @ Wout + bout

    def _L1_ffn_ref(x, w1, w2, w3):
        import jax, jax.numpy as jnp
        import numpy as np
        D_MODEL = 512
        HIDDEN = 1408
        BATCH, SEQ = (4, 512)

        def _activation_quant(x):
            scale = 127.0 / jnp.clip(jnp.max(jnp.abs(x), axis=-1, keepdims=True), 1e-05, None)
            xq = jnp.clip(jnp.round(x * scale), -128.0, 127.0) / scale
            return x + jax.lax.stop_gradient(xq - x)

        def _weight_quant(w):
            scale = 1.0 / jnp.clip(jnp.mean(jnp.abs(w)), 1e-05, None)
            wq = jnp.clip(jnp.round(w * scale), -1.0, 1.0) / scale
            return w + jax.lax.stop_gradient(wq - w)

        def _bitlinear(x, w):
            return jnp.einsum('bsi,oi->bso', _activation_quant(x), _weight_quant(w))
        h = jax.nn.silu(_bitlinear(x, w1)) * _bitlinear(x, w2)
        return _bitlinear(h, w3)
    x = x + _L0_attn_ref(_layernorm(x, axis=-1), L0_attn_conv_w, L0_attn_conv_b, L0_attn_xproj_w, L0_attn_dtproj_w, L0_attn_dtproj_b, L0_attn_A_log, L0_attn_D_skip)
    x = x + _L0_xattn_ref(_layernorm(x, axis=-1), fside_BxS2xS2_0, ctx_1024)
    x = x + _L0_ffn_ref(_layernorm(x, axis=-1), L0_ffn_W_router, L0_ffn_We_gate, L0_ffn_We_up, L0_ffn_We_down, L0_ffn_Ws_gate, L0_ffn_Ws_up, L0_ffn_Ws_down)
    x = x + _L1_attn_ref(_layernorm(x, axis=-1), L1_attn_Wq, L1_attn_Wk, L1_attn_Wv, L1_attn_conv_q_w, L1_attn_conv_q_b, L1_attn_conv_k_w, L1_attn_conv_k_b, L1_attn_conv_v_w, L1_attn_conv_v_b, L1_attn_Wfa, L1_attn_Wfb, L1_attn_A_log, L1_attn_dt_bias, L1_attn_Wb, L1_attn_Wga, L1_attn_Wgb, L1_attn_o_norm_w, L1_attn_Wo)
    x = x + _L1_xattn_ref(_layernorm(x, axis=-1), ctx_1024, fside_BxSx2_0, fside_BxSx2_0, L1_xattn_Wq, L1_xattn_Wkv, L1_xattn_Wout, L1_xattn_bout)
    x = x + _L1_ffn_ref(_layernorm(x, axis=-1), L1_ffn_w1, L1_ffn_w2, L1_ffn_w3)
    return x

_drawn_inputs = setup_inputs


def setup_inputs(seed=0):
    import zlib

    import numpy as np

    out = dict(_drawn_inputs(seed))
    spreads = {'L0_attn_conv_b': (0.0, 0.1),
     'L0_attn_dtproj_b': (0.0, 0.8),
     'L0_attn_A_log': (0.0, 0.8),
     'L0_attn_D_skip': (1.0, 0.2),
     'L1_attn_conv_q_b': (0.0, 0.1),
     'L1_attn_conv_k_b': (0.0, 0.269),
     'L1_attn_conv_v_b': (0.0, 0.277),
     'L1_attn_dt_bias': (0.0, 0.8),
     'L1_attn_o_norm_w': (1.0, 0.6),
     'L1_xattn_bout': (0.0, 0.1)}
    factors = {'fside_BxSx2_0': 8.0,
     'L0_attn_dtproj_w': 8.0,
     'L0_ffn_W_router': 6.117,
     'L0_ffn_We_gate': 5.456,
     'L0_ffn_We_up': 5.351,
     'L0_ffn_We_down': 5.338,
     'L1_attn_Wfa': 8.0,
     'L1_attn_Wfb': 8.0,
     'L1_attn_A_log': 8.0,
     'L1_attn_Wb': 4.911,
     'L1_attn_Wga': 8.0,
     'L1_attn_Wgb': 8.0,
     'L1_xattn_Wq': 8.0,
     'L1_xattn_Wkv': 6.216,
     'L1_xattn_Wout': 6.272}
    for name, (base, spread) in spreads.items():
        noise = np.random.default_rng([zlib.crc32(name.encode()), seed]).standard_normal(out[name].shape)
        drawn = base * np.exp(spread * noise) if base else spread * noise
        out[name] = jnp.asarray(drawn.astype(out[name].dtype))
    for name, factor in factors.items():
        out[name] = (out[name] * factor).astype(out[name].dtype)
    return out
```

```python
from contextlib import ExitStack

import concourse.bass as bass
from concourse import mybir

F32 = mybir.dt.float32
BF16 = mybir.dt.bfloat16
U32 = mybir.dt.uint32
U16 = mybir.dt.uint16
ALU = mybir.AluOpType
ACT = mybir.ActivationFunctionType
AX = mybir.AxisListType.X

P = 128
B, S, D = 4, 512, 512
T = B * S
NT = T // P
DT = D // P
TPB = S // P
LN_EPS = 1e-5
ROUND = 12582912.0


class Scope(ExitStack):

    def __init__(self, nc, phase):
        super().__init__()
        self.nc, self.phase = nc, phase

    def sb(self, name, shape, dt=F32):
        return self.enter_context(self.nc.sbuf_tensor(f"{self.phase}_{name}", shape, dt))

    def ps(self, name, shape, dt=F32):
        return self.enter_context(self.nc.psum_tensor(f"{self.phase}_{name}", shape, dt))

    def sem(self, name):
        return self.nc.alloc_semaphore(f"{self.phase}_{name}")


def load_constants(nc, g):
    with Scope(nc, "start") as sc:
        x_loaded = sc.sem("x_loaded")
        ident_zeroed = sc.sem("ident_zeroed")
        ident_made = sc.sem("ident_made")
        with nc.Block() as block:
            @block.sync
            def _(sp):
                sp.dma_start(g["x"][:], g["x_dram"].rearrange("(t p) d -> p t d", p=P)).then_inc(x_loaded, 16)
                sp.wait_ge(x_loaded, 16)

            @block.gpsimd
            def _(pool):
                pool.memset(g["ident"][:], 0.0).then_inc(ident_zeroed, 1)
                pool.memset(g["ones"][:], 1.0)
                pool.wait_ge(ident_zeroed, 1)
                pool.affine_select(out=g["ident"][:], in_=g["ident"][:], compare_op=ALU.not_equal, fill=1.0,
                                   base=0, pattern=[[-1, P]], channel_multiplier=1).then_inc(ident_made, 1)

            @block.vector
            def _(dve):
                dve.wait_ge(ident_made, 1)
                dve.tensor_copy(g["ident16"][:], g["ident"][:])


def store_result(nc, g):
    with Scope(nc, "end") as sc:
        x_stored = sc.sem("x_stored")
        with nc.Block() as block:
            @block.sync
            def _(sp):
                sp.dma_start(g["out_dram"].rearrange("(t p) d -> p t d", p=P), g["x"][:]).then_inc(x_stored, 16)
                sp.wait_ge(x_stored, 16)


def layer_norm(nc, g, tag, hT):
    with Scope(nc, f"norm_{tag}") as sc:
        stats = sc.sb("stats", [P, NT, 6])
        mean_var = sc.sb("mean_var", [P, NT, 2])
        rstd = sc.sb("rstd", [P, NT])
        var_ready = sc.sem("var_ready")
        std_ready = sc.sem("std_ready")
        h = sc.sb("h", [P, 2, D])
        turned = [sc.ps(f"turned{j}", [P, DT, P]) for j in range(2)]
        h_ready = sc.sem("h_ready")
        h_turned = sc.sem("h_turned")
        hT_copied = sc.sem("hT_copied")
        with nc.Block() as block:
            @block.sync
            def _(sp):
                sp.sem_inc(h_turned, 2)
                sp.sem_inc(hT_copied, 2)

            @block.vector
            def _(dve):
                with dve.Fori(0, NT) as t:
                    dve.bn_stats(stats[:, t, :], g["x"][:, t, :])
                dve.drain()
                for t in range(NT):
                    dve.bn_aggr(mean_var[:, t, :], stats[:, t, :])
                dve.drain()
                dve.tensor_scalar(rstd[:], mean_var[:, :, 1], LN_EPS, None, ALU.add).then_inc(var_ready, 1)
                dve.wait_ge(std_ready, 1)
                dve.reciprocal(rstd[:], rstd[:])
                dve.drain()
                with dve.Fori(0, NT // 2) as pair:
                    for j in range(2):
                        dve.wait_ge(h_turned, 2 * pair + j + 1)
                        dve.tensor_scalar(h[:, j, :], g["x"][:, 2 * pair + j, :], mean_var[:, 2 * pair + j, 0:1],
                                          rstd[:, bass.ds(2 * pair + j, 1)], ALU.subtract, ALU.mult).then_inc(h_ready, 1)

            @block.tensor
            def _(pe):
                with pe.Fori(0, NT // 2) as pair:
                    for j in range(2):
                        pe.wait_ge(h_ready, 2 * pair + j + 1)
                        pe.wait_ge(hT_copied, 2 * pair + j + 1)
                        for k in range(DT):
                            last = pe.transpose(turned[j][:, k, :], h[:, j, k * P:(k + 1) * P], g["ident"][:])
                        last.then_inc(h_turned, 1)

            @block.scalar
            def _(act):
                act.wait_ge(var_ready, 1)
                act.activation(rstd[:], rstd[:], ACT.Sqrt).then_inc(std_ready, 1)
                with act.Fori(0, NT // 2) as pair:
                    for j in range(2):
                        act.wait_ge(h_turned, 2 + 2 * pair + j + 1)
                        act.activation(hT[:, :, bass.ds((2 * pair + j) * P, P)], turned[j][:],
                                       ACT.Copy).then_inc(hT_copied, 1)


def normalize_rows(nc, g, tag, h):
    with Scope(nc, f"rows_{tag}") as sc:
        stats = sc.sb("stats", [P, NT, 6])
        mean_var = sc.sb("mean_var", [P, NT, 2])
        rstd = sc.sb("rstd", [P, NT])
        var_ready = sc.sem("var_ready")
        std_ready = sc.sem("std_ready")
        with nc.Block() as block:
            @block.scalar
            def _(act):
                act.wait_ge(var_ready, 1)
                act.activation(rstd[:], rstd[:], ACT.Sqrt).then_inc(std_ready, 1)

            @block.vector
            def _(dve):
                with dve.Fori(0, NT) as t:
                    dve.bn_stats(stats[:, t, :], g["x"][:, t, :])
                dve.drain()
                for t in range(NT):
                    dve.bn_aggr(mean_var[:, t, :], stats[:, t, :])
                dve.drain()
                dve.tensor_scalar(rstd[:], mean_var[:, :, 1], LN_EPS, None, ALU.add).then_inc(var_ready, 1)
                dve.wait_ge(std_ready, 1)
                dve.reciprocal(rstd[:], rstd[:])
                dve.drain()
                with dve.Fori(0, NT) as t:
                    dve.tensor_scalar(h[:, t, :], g["x"][:, t, :], mean_var[:, t, 0:1],
                                      rstd[:, bass.ds(t, 1)], ALU.subtract, ALU.mult)



STATE, RANK, TAPS = 16, 128, 4


def selective_scan_layer(nc, g):
    with Scope(nc, "scan") as outer:
        hT = outer.sb("hT", [P, DT, T])
        uT = outer.sb("uT", [P, DT, T])
        conv_w = outer.sb("conv_w", [P, DT, TAPS])
        conv_b = outer.sb("conv_b", [P, DT])
        dt_b = outer.sb("dt_b", [P, DT])
        a_neg = outer.sb("a_neg", [P, DT, STATE])
        d_skip = outer.sb("d_skip", [P, DT])
        layer_norm(nc, g, "scan", hT)

        with Scope(nc, "conv") as sc:
            params_loaded = sc.sem("params_loaded")
            a_loaded = sc.sem("a_loaded")
            a_exp = sc.sem("a_exp")
            with nc.Block() as block:
                @block.sync
                def _(sp):
                    sp.dma_start(conv_w[:], g["conv_w"].rearrange("(k p) j -> p k j", p=P)).then_inc(params_loaded, 16)
                    sp.dma_start(conv_b[:], g["conv_b"]).then_inc(params_loaded, 16)
                    sp.dma_start(dt_b[:], g["dt_b"]).then_inc(params_loaded, 16)
                    sp.dma_start(d_skip[:], g["d_skip"]).then_inc(params_loaded, 16)
                    sp.dma_start(a_neg[:], g["a_log"].rearrange("(k p) n -> p k n", p=P)).then_inc(a_loaded, 16)
                    sp.wait_ge(params_loaded, 64)
                    sp.wait_ge(a_loaded, 16)

                @block.scalar
                def _(act):
                    act.wait_ge(a_loaded, 16)
                    act.activation(a_neg[:], a_neg[:], ACT.Exp).then_inc(a_exp, 1)

                @block.vector
                def _(dve):
                    dve.wait_ge(params_loaded, 64)
                    for k in range(DT):
                        h = hT[:, k, :].rearrange("p (b s) -> p b s", b=B)
                        u = uT[:, k, :].rearrange("p (b s) -> p b s", b=B)
                        dve.tensor_scalar(u, h, conv_w[:, k, TAPS - 1:TAPS], conv_b[:, k:k + 1], ALU.mult, ALU.add)
                    for back in range(1, TAPS):
                        dve.drain()
                        for k in range(DT):
                            h = hT[:, k, :].rearrange("p (b s) -> p b s", b=B)[:, :, 0:S - back]
                            u = uT[:, k, :].rearrange("p (b s) -> p b s", b=B)[:, :, back:S]
                            dve.scalar_tensor_tensor(u, h, conv_w[:, k, TAPS - 1 - back:TAPS - back], u,
                                                     ALU.mult, ALU.add)
                    dve.wait_ge(a_exp, 1)
                    dve.tensor_scalar(a_neg[:], a_neg[:], -1.0, None, ALU.mult)

        delta = hT
        with Scope(nc, "delta") as sc:
            xproj = sc.sb("xproj", [P, DT, RANK + 2 * STATE])
            dtproj = sc.sb("dtproj", [P, D])
            dtT = sc.sb("dtT", [RANK, T])
            bcT = sc.sb("bcT", [2 * STATE, T])
            z = sc.sb("z", [P, 2, T])
            az = sc.sb("az", [P, 2, T])
            e = sc.sb("e", [P, 2, T])
            u1 = sc.sb("u1", [P, 2, T])
            lnu = az
            dt_ps = [sc.ps(f"dt_ps{c}", [RANK, S]) for c in range(2)]
            bc_ps = [sc.ps(f"bc_ps{c}", [2 * STATE, S]) for c in range(2)]
            z_ps = [sc.ps(f"z_ps{c}", [P, S]) for c in range(B)]
            w_loaded = sc.sem("w_loaded")
            dt_done = sc.sem("dt_done")
            bc_done = sc.sem("bc_done")
            dt_copied = sc.sem("dt_copied")
            z_done = sc.sem("z_done")
            z_read = sc.sem("z_read")
            abs_done = sc.sem("abs_done")
            exp_done = sc.sem("exp_done")
            u1_done = sc.sem("u1_done")
            ln_done = sc.sem("ln_done")
            delta_done = sc.sem("delta_done")
            bc_stored = sc.sem("bc_stored")
            with nc.Block() as block:
                @block.sync
                def _(sp):
                    sp.dma_start(xproj[:], g["xproj_wT"].rearrange("(k p) e -> p k e", p=P)).then_inc(w_loaded, 16)
                    sp.dma_start(dtproj[:], g["dtproj_wT"]).then_inc(w_loaded, 16)
                    sp.wait_ge(dt_copied, 2 * B)
                    sp.dma_start(g["bc_dram"], bcT[:]).then_inc(bc_stored, 16)
                    sp.wait_ge(bc_stored, 16)

                @block.tensor
                def _(pe):
                    pe.wait_ge(w_loaded, 32)
                    for c in range(B):
                        if c >= 2:
                            pe.wait_ge(dt_copied, 2 * (c - 1))
                        for k in range(DT):
                            last = pe.matmul(dt_ps[c % 2][:], xproj[:, k, 0:RANK], uT[:, k, c * S:(c + 1) * S],
                                             start=(k == 0), stop=(k == DT - 1))
                        last.then_inc(dt_done, 1)
                        for k in range(DT):
                            last = pe.matmul(bc_ps[c % 2][:], xproj[:, k, RANK:RANK + 2 * STATE],
                                             uT[:, k, c * S:(c + 1) * S], start=(k == 0), stop=(k == DT - 1))
                        last.then_inc(bc_done, 1)
                    pe.wait_ge(dt_copied, 2 * B)
                    for k in range(DT):
                        for c in range(B):
                            if k > 0:
                                pe.wait_ge(z_read, (k - 1) * B + c + 1)
                            pe.matmul(z_ps[c][:], dtproj[:, k * P:(k + 1) * P], dtT[:, c * S:(c + 1) * S],
                                      start=True, stop=True).then_inc(z_done, 1)

                @block.scalar
                def _(act):
                    for c in range(B):
                        act.wait_ge(dt_done, c + 1)
                        act.activation(dtT[:, c * S:(c + 1) * S], dt_ps[c % 2][:], ACT.Copy).then_inc(dt_copied, 1)
                        act.wait_ge(bc_done, c + 1)
                        act.activation(bcT[:, c * S:(c + 1) * S], bc_ps[c % 2][:], ACT.Copy).then_inc(dt_copied, 1)
                    for k in range(DT):
                        act.wait_ge(abs_done, k + 1)
                        act.activation(e[:, k % 2, :], az[:, k % 2, :], ACT.Exp, scale=-1.0).then_inc(exp_done, 1)
                        act.wait_ge(u1_done, k + 1)
                        act.activation(lnu[:, k % 2, :], u1[:, k % 2, :], ACT.Ln).then_inc(ln_done, 1)

                @block.vector
                def _(dve):
                    def magnitude(k):
                        j = k % 2
                        for c in range(B):
                            dve.wait_ge(z_done, k * B + c + 1)
                            dve.tensor_scalar(z[:, j, c * S:(c + 1) * S], z_ps[c][:], dt_b[:, k:k + 1], None, ALU.add).then_inc(z_read, 1)
                        dve.drain()
                        dve.scalar_tensor_tensor(az[:, j, :], z[:, j, :], -1.0, z[:, j, :], ALU.mult, ALU.max).then_inc(abs_done, 1)

                    def one_plus(k):
                        j = k % 2
                        dve.wait_ge(exp_done, k + 1)
                        dve.tensor_scalar(u1[:, j, :], e[:, j, :], 1.0, None, ALU.add).then_inc(u1_done, 1)
                        dve.drain()
                        dve.scalar_tensor_tensor(e[:, j, :], u1[:, j, :], 1.0, e[:, j, :], ALU.subtract, ALU.subtract)

                    def finish(k):
                        j = k % 2
                        dve.wait_ge(ln_done, k + 1)
                        dve.scalar_tensor_tensor(lnu[:, j, :], u1[:, j, :], 1.0, lnu[:, j, :], ALU.is_gt, ALU.mult)
                        dve.drain()
                        dve.tensor_tensor(lnu[:, j, :], lnu[:, j, :], e[:, j, :], ALU.subtract)
                        dve.drain()
                        dve.scalar_tensor_tensor(delta[:, k, :], z[:, j, :], 0.0, lnu[:, j, :], ALU.max, ALU.add)
                        dve.drain()

                    magnitude(0)
                    for k in range(DT):
                        one_plus(k)
                        if k + 1 < DT:
                            magnitude(k + 1)
                        finish(k)

        NBUF = 4
        with Scope(nc, "states") as sc:
            bc = sc.sb("bc", [P, 2 * STATE, S])
            d_diag = sc.sb("d_diag", [P, DT, P])
            du = sc.sb("du", [P, S])
            steps = sc.sb("steps", [P, S])
            decay = sc.sb("decay", [P, NBUF, S])
            inp = sc.sb("inp", [P, NBUF, S])
            hs = sc.sb("hs", [P, NBUF, S])
            hc = sc.sb("hc", [P, NBUF, S])
            y = sc.sb("y", [P, 2, S])
            y_ps = [sc.ps(f"y_ps{j}", [P, S]) for j in range(2)]
            yT_ps = [sc.ps(f"yT_ps{j}", [P, TPB, P]) for j in range(2)]
            bc_loaded = [sc.sem(f"bc_loaded{n}") for n in range(STATE)]
            d_ready = sc.sem("d_ready")
            du_done = sc.sem("du_done")
            decay_done = sc.sem("decay_done")
            inp_done = sc.sem("inp_done")
            scanned = sc.sem("scanned")
            hc_done = sc.sem("hc_done")
            hc_summed = sc.sem("hc_summed")
            y_copied = sc.sem("y_copied")
            y_turned = sc.sem("y_turned")
            y_added = sc.sem("y_added")
            with nc.Block() as block:
                @block.sync
                def _(sp):
                    sp.sem_inc(scanned, NBUF)
                    sp.sem_inc(hc_summed, NBUF)
                    sp.sem_inc(hc_done, STATE)
                    sp.sem_inc(y_added, 2)
                    sp.sem_inc(y_copied, 2)
                    with sp.Fori(0, B) as b:
                        for n in range(STATE):
                            sp.wait_ge(hc_done, b * DT * STATE + n + 1)
                            for row in (n, STATE + n):
                                src = g["bc_dram"][row:row + 1, bass.ds(b * S, S)]
                                sp.dma_start(bc[:, row, :], src.to_broadcast([P, S])).then_inc(bc_loaded[n], 16)
                    for n in range(STATE):
                        sp.wait_ge(bc_loaded[n], 32 * B)

                @block.scalar
                def _(act):
                    with act.Fori(0, B) as b:
                        def copy_y(k):
                            act.wait_ge(hc_summed, NBUF + (b * DT + k + 1) * STATE)
                            act.wait_ge(y_turned, b * DT + k)
                            act.activation(y[:, k % 2, :], y_ps[k % 2][:], ACT.Copy).then_inc(y_copied, 1)

                        for k in range(DT):
                            m = (b * DT + k) * STATE
                            act.drain()
                            act.activation(steps[:], delta[:, k, bass.ds(b * S, S)], ACT.Copy)
                            act.drain()
                            for n in range(STATE):
                                act.wait_ge(scanned, m + n + 1)
                                act.activation(decay[:, n % NBUF, :], steps[:], ACT.Exp,
                                               scale=a_neg[:, k, n:n + 1]).then_inc(decay_done, 1)
                                if n == NBUF and k > 0:
                                    copy_y(k - 1)
                        copy_y(DT - 1)

                @block.gpsimd
                def _(pool):
                    with pool.Fori(0, B) as b:
                        for k in range(DT):
                            m = (b * DT + k) * STATE
                            pool.wait_ge(scanned, NBUF + m)
                            pool.tensor_tensor(du[:], delta[:, k, bass.ds(b * S, S)], uT[:, k, bass.ds(b * S, S)],
                                               ALU.mult).then_inc(du_done, 1)
                            pool.wait_ge(du_done, b * DT + k + 1)
                            for n in range(STATE):
                                if k == 0:
                                    pool.wait_ge(bc_loaded[n], 32 * (b + 1))
                                pool.wait_ge(scanned, m + n + 1)
                                pool.tensor_tensor(inp[:, n % NBUF, :], du[:], bc[:, n, :],
                                                   ALU.mult).then_inc(inp_done, 1)

                @block.vector
                def _(dve):
                    for k in range(DT):
                        last = dve.tensor_scalar(d_diag[:, k, :], g["ident"][:], d_skip[:, k:k + 1], None, ALU.mult)
                    last.then_inc(d_ready, 1)
                    with dve.Fori(0, B) as b:
                        def weigh(m, n):
                            dve.wait_ge(scanned, NBUF + m + n + 1)
                            dve.wait_ge(hc_summed, m + n + 1)
                            dve.tensor_tensor(hc[:, n % NBUF, :], hs[:, n % NBUF, :], bc[:, STATE + n, :],
                                              ALU.mult).then_inc(hc_done, 1)

                        def add(k):
                            xs = g["x"][:, bass.ds(b * TPB, TPB), k * P:(k + 1) * P]
                            dve.wait_ge(y_turned, b * DT + k + 1)
                            dve.tensor_tensor(xs, yT_ps[k % 2][:], xs, ALU.add).then_inc(y_added, 1)

                        for k in range(DT):
                            m = (b * DT + k) * STATE
                            for n in range(STATE):
                                if k == 0:
                                    dve.wait_ge(bc_loaded[n], 32 * (b + 1))
                                dve.wait_ge(hc_done, STATE + m + n + 1 - NBUF)
                                dve.wait_ge(decay_done, m + n + 1)
                                dve.wait_ge(inp_done, m + n + 1)
                                dve.tensor_tensor_scan(hs[:, n % NBUF, :], decay[:, n % NBUF, :],
                                                       inp[:, n % NBUF, :], 0.0, ALU.mult, ALU.add).then_inc(scanned, 1)
                                if n > 0:
                                    weigh(m, n - 1)
                                if n == 2 * NBUF and k > 0:
                                    add(k - 1)
                            weigh(m, STATE - 1)
                        add(DT - 1)

                @block.tensor
                def _(pe):
                    pe.wait_ge(d_ready, 1)
                    with pe.Fori(0, B) as b:
                        def turn(k):
                            i = b * DT + k
                            pe.wait_ge(y_copied, 2 + i + 1)
                            pe.wait_ge(y_added, i + 1)
                            for t in range(TPB):
                                last = pe.transpose(yT_ps[k % 2][:, t, :], y[:, k % 2, t * P:(t + 1) * P], g["ident"][:])
                            last.then_inc(y_turned, 1)

                        for k in range(DT):
                            i = b * DT + k
                            pe.wait_ge(y_copied, i + 1)
                            pe.matmul(y_ps[k % 2][:], d_diag[:, k, :], uT[:, k, bass.ds(b * S, S)], start=True, stop=False)
                            for n in range(STATE):
                                pe.wait_ge(hc_done, STATE + i * STATE + n + 1)
                                last = pe.matmul(y_ps[k % 2][:], g["ident"][:], hc[:, n % NBUF, :], start=False, stop=(n == STATE - 1))
                                last.then_inc(hc_summed, 1)
                                if n == NBUF + 2 and k > 0:
                                    turn(k - 1)
                        turn(DT - 1)



QMAX, QEPS = 127.0, 1e-6
INNER = 256


def smooth_quant_layer(nc, g):
    with Scope(nc, "sq_h") as outer:
        hT = outer.sb("hT", [P, DT, T])
        layer_norm(nc, g, "sq", hT)
        KT = (DT, INNER // P)
        with Scope(nc, "sq") as sc:
            w = [sc.sb("w_in", [P, KT[0], S]), sc.sb("w_out", [P, KT[1], S])]
            xs = sc.sb("xs", [P, DT, S])
            ws = sc.sb("ws", [P, DT, S])
            xmax = sc.sb("xmax", [P, DT])
            wmax = sc.sb("wmax", [P, DT])
            smooth = sc.sb("smooth", [P, DT])
            unsmooth = sc.sb("unsmooth", [P, DT])
            row_scale = [sc.sb("x_scale", [P, TPB]), sc.sb("w_scale", [P, TPB])]
            row_inv = sc.sb("row_inv", [P, TPB])
            rounded = sc.sb("rounded", [P, 2, D])
            q_rows = sc.sb("q_rows", [P, TPB, D], BF16)
            qT = [sc.sb("xqT", [P, DT, S], BF16), sc.sb("wqT", [P, DT, S], BF16)]
            spread = sc.sb("spread", [P, TPB, P])
            scale_row = sc.sb("scale_row", [P, S])
            gate = sc.sb("gate", [P, KT[1], S])
            silu = sc.sb("silu", [P, KT[1], S])
            up = sc.sb("up", [P, KT[1], S])
            actT = sc.sb("actT", [P, KT[1], S])
            back = sc.sb("back", [P, S])
            rows_ps = [sc.ps(f"rows_ps{r}", [P, D]) for r in range(TPB)]
            q_ps = [sc.ps(f"q_ps{j}", [P, 2, S], BF16) for j in range(2)]
            acc = [sc.ps(f"acc{j}", [P, S]) for j in range(2)]
            w_loaded = sc.sem("w_loaded")
            smooth_sq = sc.sem("smooth_sq")
            smooth_root = sc.sem("smooth_root")
            scaled = sc.sem("scaled")
            rows_turned = sc.sem("rows_turned")
            quantized = sc.sem("quantized")
            q_turned = sc.sem("q_turned")
            q_copied = sc.sem("q_copied")
            spread_done = sc.sem("spread_done")
            scale_row_done = sc.sem("scale_row_done")
            scale_row_copied = sc.sem("scale_row_copied")
            acc_done = sc.sem("acc_done")
            acc_read = sc.sem("acc_read")
            silu_done = sc.sem("silu_done")
            with nc.Block() as block:
                @block.sync
                def _(sp):
                    sp.sem_inc(acc_read, 2)
                    with sp.Fori(0, B) as b:
                        sp.wait_ge(scaled, 2 * b)
                        sp.dma_start(w[0][:], g["gate_up_T"][b].rearrange("(k p) o -> p k o", p=P)).then_inc(w_loaded, 16)
                        sp.dma_start(w[1][:], g["down_T"][b].rearrange("(k p) o -> p k o", p=P)).then_inc(w_loaded, 16)
                    sp.wait_ge(w_loaded, 32 * B)

                @block.vector
                def _(dve):
                    def quantize(of, width, done):
                        dve.wait_ge(rows_turned, done + 1)
                        for r in range(TPB):
                            dve.tensor_reduce(row_scale[of][:, r:r + 1], rows_ps[r][:, 0:width], AX, ALU.max,
                                              apply_absolute_value=True)
                        dve.drain()
                        dve.tensor_scalar(row_scale[of][:], row_scale[of][:], QEPS, 1.0 / QMAX, ALU.max, ALU.mult)
                        dve.drain()
                        dve.reciprocal(row_inv[:], row_scale[of][:])
                        dve.drain()
                        dve.wait_ge(q_turned, done)
                        for r in range(TPB):
                            dve.tensor_scalar(rounded[:, r % 2, 0:width], rows_ps[r][:, 0:width],
                                              row_inv[:, r:r + 1], ROUND, ALU.mult, ALU.add)
                            dve.drain()
                            last = dve.tensor_scalar(q_rows[:, r, 0:width], rounded[:, r % 2, 0:width],
                                                     ROUND, None, ALU.subtract)
                        last.then_inc(quantized, 1)

                    with dve.Fori(0, B) as b:
                        for lin in range(2):
                            n = KT[lin]
                            u = 2 * b + lin
                            x = hT[:, :, bass.ds(b * S, S)] if lin == 0 else actT[:]
                            dve.drain()
                            dve.wait_ge(w_loaded, 32 * (b + 1))
                            dve.tensor_reduce(xmax[:, 0:n], x, AX, ALU.max, apply_absolute_value=True)
                            dve.tensor_reduce(wmax[:, 0:n], w[lin][:], AX, ALU.max, apply_absolute_value=True)
                            dve.drain()
                            dve.tensor_scalar(xmax[:, 0:n], xmax[:, 0:n], QEPS, None, ALU.max)
                            dve.tensor_scalar(wmax[:, 0:n], wmax[:, 0:n], QEPS, None, ALU.max)
                            dve.drain()
                            dve.reciprocal(wmax[:, 0:n], wmax[:, 0:n])
                            dve.drain()
                            dve.tensor_tensor(smooth[:, 0:n], xmax[:, 0:n], wmax[:, 0:n], ALU.mult).then_inc(smooth_sq, 1)
                            dve.wait_ge(smooth_root, u + 1)
                            dve.tensor_scalar(smooth[:, 0:n], smooth[:, 0:n], QEPS, None, ALU.max)
                            dve.drain()
                            dve.reciprocal(unsmooth[:, 0:n], smooth[:, 0:n])
                            dve.drain()
                            for k in range(n):
                                xk = hT[:, k, bass.ds(b * S, S)] if lin == 0 else actT[:, k, :]
                                dve.tensor_scalar(xs[:, k, :], xk, unsmooth[:, k:k + 1], None, ALU.mult)
                                last = dve.tensor_scalar(ws[:, k, :], w[lin][:, k, :], smooth[:, k:k + 1], None, ALU.mult)
                            last.then_inc(scaled, 1)
                            quantize(0, n * P, 2 * u)
                            quantize(1, n * P, 2 * u + 1)
                            along = row_scale[0] if lin == 0 else row_scale[1]
                            across = row_scale[1] if lin == 0 else row_scale[0]
                            dve.wait_ge(scale_row_done, u)
                            for r in range(TPB):
                                last = dve.tensor_scalar(spread[:, r, :], g["ones"][:], along[:, r:r + 1], None, ALU.mult)
                            last.then_inc(spread_done, 1)
                            dve.wait_ge(scale_row_copied, u + 1)
                            for r in range(TPB):
                                dve.wait_ge(acc_done, TPB * u + r + 1)
                                if lin == 0:
                                    to = gate[:, r, :] if r < KT[1] else up[:, r - KT[1], :]
                                    dve.scalar_tensor_tensor(to, acc[r % 2][:], across[:, r:r + 1], scale_row[:],
                                                             ALU.mult, ALU.mult).then_inc(acc_read, 1)
                                else:
                                    dve.scalar_tensor_tensor(back[:], acc[r % 2][:], across[:, r:r + 1], scale_row[:],
                                                             ALU.mult, ALU.mult).then_inc(acc_read, 1)
                                    dve.drain()
                                    xr = g["x"][:, bass.ds(b * TPB + r, 1), :].rearrange("p o d -> p (o d)")
                                    dve.tensor_tensor(xr, xr, back[:], ALU.add)
                                    dve.drain()
                            if lin == 0:
                                dve.drain()
                                dve.wait_ge(silu_done, b + 1)
                                dve.tensor_tensor(actT[:], silu[:], up[:], ALU.mult)

                @block.scalar
                def _(act):
                    def copy_turned(of, n, done):
                        act.wait_ge(q_turned, done + 1)
                        for j in range(n // 2):
                            last = act.activation(qT[of][:, 2 * j:2 * j + 2, :], q_ps[j][:], ACT.Copy)
                        last.then_inc(q_copied, 1)

                    with act.Fori(0, B) as b:
                        for lin in range(2):
                            u = 2 * b + lin
                            act.wait_ge(smooth_sq, u + 1)
                            act.activation(smooth[:, 0:KT[lin]], smooth[:, 0:KT[lin]], ACT.Sqrt).then_inc(smooth_root, 1)
                            copy_turned(0, KT[lin], 2 * u)
                            copy_turned(1, KT[lin], 2 * u + 1)
                            act.wait_ge(scale_row_done, u + 1)
                            act.wait_ge(acc_read, 2 + TPB * u)
                            act.activation(scale_row[:], rows_ps[0][:, 0:S], ACT.Copy).then_inc(scale_row_copied, 1)
                            if lin == 0:
                                act.wait_ge(acc_read, 2 + TPB * u + KT[1])
                                act.activation(silu[:], gate[:], ACT.Silu).then_inc(silu_done, 1)

                @block.tensor
                def _(pe):
                    def turn_rows(src, n):
                        for r in range(TPB):
                            for k in range(n):
                                last = pe.transpose(rows_ps[r][:, k * P:(k + 1) * P], src[:, k, r * P:(r + 1) * P],
                                                    g["ident"][:])
                        last.then_inc(rows_turned, 1)

                    def turn_back(n):
                        for k in range(n):
                            for r in range(TPB):
                                last = pe.transpose(q_ps[k // 2][:, k % 2, r * P:(r + 1) * P],
                                                    q_rows[:, r, k * P:(k + 1) * P], g["ident16"][:])
                        last.then_inc(q_turned, 1)

                    with pe.Fori(0, B) as b:
                        for lin in range(2):
                            n = KT[lin]
                            u = 2 * b + lin
                            pe.wait_ge(scaled, u + 1)
                            pe.wait_ge(scale_row_copied, u)
                            turn_rows(xs, n)
                            pe.wait_ge(quantized, 2 * u + 1)
                            turn_rows(ws, n)
                            pe.wait_ge(q_copied, 2 * u)
                            turn_back(n)
                            pe.wait_ge(quantized, 2 * u + 2)
                            pe.wait_ge(q_copied, 2 * u + 1)
                            turn_back(n)
                            pe.wait_ge(spread_done, u + 1)
                            for r in range(TPB):
                                last = pe.matmul(rows_ps[0][:, r * P:(r + 1) * P], spread[:, r, :], g["ident"][:],
                                                 start=True, stop=True)
                            last.then_inc(scale_row_done, 1)
                            pe.wait_ge(q_copied, 2 * u + 2)
                            left, right = (qT[1], qT[0]) if lin == 0 else (qT[0], qT[1])
                            for r in range(TPB):
                                pe.wait_ge(acc_read, TPB * u + r + 1)
                                for k in range(n):
                                    last = pe.matmul(acc[r % 2][:], left[:, k, r * P:(r + 1) * P], right[:, k, :],
                                                     start=(k == 0), stop=(k == n - 1))
                                last.then_inc(acc_done, 1)



EXPERTS, TOP_K, HIDDEN = 8, 2, 352
ALL_EXPERTS = EXPERTS + 2
HIDDEN_TILES = [(m, min(P, HIDDEN - m)) for m in range(0, HIDDEN, P)]
HT = len(HIDDEN_TILES)


def expert_layer(nc, g):
    with Scope(nc, "moe") as outer:
        hT = outer.sb("hT", [P, DT, T])
        combine = outer.sb("combine", [P, NT, ALL_EXPERTS])
        layer_norm(nc, g, "moe", hT)

        with Scope(nc, "router") as sc:
            w_router = sc.sb("w_router", [P, DT, EXPERTS])
            top = sc.sb("top", [P, NT])
            score = sc.sb("score", [P, NT, EXPERTS])
            total = sc.sb("total", [P, NT])
            ahead = sc.sb("ahead", [P, NT, EXPERTS, EXPERTS])
            equal = sc.sb("equal", [P, NT, EXPERTS, EXPERTS])
            earlier = sc.sb("earlier", [P, EXPERTS, EXPERTS])
            rank = sc.sb("rank", [P, NT, EXPERTS])
            logits = sc.ps("logits", [P, NT, EXPERTS])
            router_loaded = sc.sem("router_loaded")
            logits_done = sc.sem("logits_done")
            shifted = sc.sem("shifted")
            exp_done = sc.sem("exp_done")
            earlier_ones = sc.sem("earlier_ones")
            earlier_done = sc.sem("earlier_done")
            with nc.Block() as block:
                @block.sync
                def _(sp):
                    sp.dma_start(w_router[:], g["w_router"].rearrange("(k p) e -> p k e", p=P)).then_inc(router_loaded, 16)
                    sp.wait_ge(router_loaded, 16)

                @block.gpsimd
                def _(pool):
                    pool.memset(earlier[:], 1.0).then_inc(earlier_ones, 1)
                    pool.wait_ge(earlier_ones, 1)
                    pool.affine_select(out=earlier[:], in_=earlier[:], compare_op=ALU.is_gt, fill=0.0, base=0,
                                       pattern=[[1, EXPERTS], [-1, EXPERTS]], channel_multiplier=0).then_inc(earlier_done, 1)

                @block.tensor
                def _(pe):
                    pe.wait_ge(router_loaded, 16)
                    for t in range(NT):
                        for k in range(DT):
                            last = pe.matmul(logits[:, t, :], hT[:, k, t * P:(t + 1) * P], w_router[:, k, :],
                                             start=(k == 0), stop=(k == DT - 1))
                    last.then_inc(logits_done, 1)

                @block.scalar
                def _(act):
                    act.wait_ge(shifted, 1)
                    act.activation(score[:], score[:], ACT.Exp).then_inc(exp_done, 1)

                @block.vector
                def _(dve):
                    dve.wait_ge(logits_done, 1)
                    dve.tensor_reduce(top[:], logits[:], AX, ALU.max)
                    dve.drain()
                    dve.tensor_tensor(score[:], logits[:], top[:].unsqueeze(2).to_broadcast([P, NT, EXPERTS]),
                                      ALU.subtract).then_inc(shifted, 1)
                    dve.wait_ge(exp_done, 1)
                    dve.tensor_reduce(total[:], score[:], AX, ALU.add)
                    dve.drain()
                    dve.reciprocal(total[:], total[:])
                    dve.drain()
                    dve.tensor_tensor(score[:], score[:], total[:].unsqueeze(2).to_broadcast([P, NT, EXPERTS]), ALU.mult)
                    dve.drain()
                    dve.wait_ge(earlier_done, 1)
                    shape = [P, NT, EXPERTS, EXPERTS]
                    mine = score[:].unsqueeze(3).to_broadcast(shape)
                    theirs = score[:].unsqueeze(2).to_broadcast(shape)
                    dve.tensor_tensor(ahead[:], theirs, mine, ALU.is_gt)
                    dve.tensor_tensor(equal[:], theirs, mine, ALU.is_equal)
                    dve.drain()
                    dve.tensor_tensor(equal[:], equal[:], earlier[:].unsqueeze(1).to_broadcast(shape), ALU.mult)
                    dve.drain()
                    dve.tensor_tensor(ahead[:], ahead[:], equal[:], ALU.add)
                    dve.drain()
                    dve.tensor_reduce(rank[:], ahead[:], AX, ALU.add)
                    dve.drain()
                    dve.scalar_tensor_tensor(combine[:, :, 0:EXPERTS], rank[:], float(TOP_K), score[:],
                                             ALU.is_lt, ALU.mult)
                    dve.memset(combine[:, :, EXPERTS:ALL_EXPERTS], 1.0)

        with Scope(nc, "experts") as sc:
            wg = [sc.sb(f"wg{j}", [P, DT, HIDDEN]) for j in range(2)]
            wu = [sc.sb(f"wu{j}", [P, DT, HIDDEN]) for j in range(2)]
            wd = [sc.sb(f"wd{j}", [P, HT, D]) for j in range(2)]
            silu = sc.sb("silu", [P, 2, S])
            actT = sc.sb("actT", [P, 2, HT, S])
            gate_ps = [sc.ps(f"gate_ps{j}", [P, S]) for j in range(2)]
            up_ps = [sc.ps(f"up_ps{j}", [P, S]) for j in range(2)]
            out_ps = [sc.ps(f"out_ps{j}", [P, D]) for j in range(TPB)]
            w_loaded = [sc.sem(f"w_loaded{j}") for j in range(2)]
            hidden_done = sc.sem("hidden_done")
            silu_done = sc.sem("silu_done")
            act_done = sc.sem("act_done")
            out_done = sc.sem("out_done")
            out_added = sc.sem("out_added")
            PER = B * TPB
            last_rows = HIDDEN_TILES[-1][1]

            with nc.Block() as block:
                @block.sync
                def _(sp):
                    sp.sem_inc(act_done, 2)
                    sp.sem_inc(out_added, TPB)
                    sp.sem_inc(out_done, 2 * PER)
                    with sp.Fori(0, ALL_EXPERTS // 2) as pair:
                        for j in range(2):
                            e = 2 * pair + j
                            sp.wait_ge(out_done, PER * (e + 1))
                            for w, src in ((wg[j], g["w_gate"]), (wu[j], g["w_up"])):
                                sp.dma_start(w[:], src[e].rearrange("(k p) h -> p k h", p=P)).then_inc(w_loaded[j], 16)
                            sp.dma_start(wd[j][:, 0:HT - 1, :], g["w_down"][e, 0:(HT - 1) * P, :].rearrange(
                                "(m p) d -> p m d", p=P)).then_inc(w_loaded[j], 16)
                            sp.dma_start(wd[j][0:last_rows, HT - 1, :], g["w_down"][e, (HT - 1) * P:HIDDEN, :]).then_inc(w_loaded[j], 16)
                    for j in range(2):
                        sp.wait_ge(w_loaded[j], 64 * (ALL_EXPERTS // 2))

                @block.tensor
                def _(pe):
                    with pe.Fori(0, ALL_EXPERTS // 2) as pair:
                        for j in range(2):
                            e = 2 * pair + j

                            def hidden(c):
                                for m, (lo, rows) in enumerate(HIDDEN_TILES):
                                    n = (e * B + c) * HT + m
                                    pe.wait_ge(act_done, n + 1)
                                    for w, to in ((wg[j], gate_ps), (wu[j], up_ps)):
                                        for k in range(DT):
                                            last = pe.matmul(to[(c * HT + m) % 2][0:rows, :], w[:, k, lo:lo + rows],
                                                             hT[:, k, c * S:(c + 1) * S], start=(k == 0), stop=(k == DT - 1))
                                    last.then_inc(hidden_done, 1)

                            def down(c):
                                pe.wait_ge(act_done, 2 + (e * B + c + 1) * HT)
                                for t in range(TPB):
                                    pe.wait_ge(out_added, (e * B + c) * TPB + t + 1)
                                    for m, (lo, rows) in enumerate(HIDDEN_TILES):
                                        last = pe.matmul(out_ps[t][:], actT[0:rows, c % 2, m, t * P:(t + 1) * P],
                                                         wd[j][0:rows, m, :], start=(m == 0), stop=(m == HT - 1))
                                    last.then_inc(out_done, 1)

                            pe.wait_ge(w_loaded[j], 64 * (pair + 1))
                            hidden(0)
                            for c in range(1, B):
                                hidden(c)
                                down(c - 1)
                            down(B - 1)

                @block.scalar
                def _(act):
                    with act.Fori(0, ALL_EXPERTS) as e:
                        for c in range(B):
                            for m, (lo, rows) in enumerate(HIDDEN_TILES):
                                n = (e * B + c) * HT + m
                                act.wait_ge(hidden_done, n + 1)
                                act.wait_ge(act_done, n + 1)
                                act.activation(silu[0:rows, (c * HT + m) % 2, :], gate_ps[(c * HT + m) % 2][0:rows, :],
                                               ACT.Silu).then_inc(silu_done, 1)

                @block.vector
                def _(dve):
                    with dve.Fori(0, ALL_EXPERTS) as e:
                        def gated(c):
                            dve.wait_ge(out_done, 2 * PER + (e * B + c) * TPB - TPB if c else 2 * PER + e * PER - TPB)
                            for m, (lo, rows) in enumerate(HIDDEN_TILES):
                                n = (e * B + c) * HT + m
                                dve.wait_ge(silu_done, n + 1)
                                dve.tensor_tensor(actT[0:rows, c % 2, m, :], silu[0:rows, (c * HT + m) % 2, :],
                                                  up_ps[(c * HT + m) % 2][0:rows, :], ALU.mult).then_inc(act_done, 1)

                        def add(c):
                            for t in range(TPB):
                                i = c * TPB + t
                                dve.wait_ge(out_done, 2 * PER + (e * B + c) * TPB + t + 1)
                                dve.scalar_tensor_tensor(g["x"][:, i, :], out_ps[t][:], combine[:, i, bass.ds(e, 1)],
                                                         g["x"][:, i, :], ALU.mult, ALU.add).then_inc(out_added, 1)

                        gated(0)
                        for c in range(1, B):
                            gated(c)
                            add(c - 1)
                        add(B - 1)
                        dve.drain()



HEADS, K = 16, 128
L2_EPS, O_EPS = 1e-6, 1e-5
CHUNK = P
CHUNKS = S // CHUNK
HALVES = [1, 2, 4, 8, 16, 32, 64]
SMALL = 16


def delta_rule_layer(nc, g):
    with Scope(nc, "kda") as outer:
        hT = outer.sb("hT", [P, DT, T])
        faT = outer.sb("faT", [P, T])
        gaT = outer.sb("gaT", [P, T])
        neg_a = outer.sb("neg_a", [P, HEADS])
        layer_norm(nc, g, "kda", hT)
        low_rank(nc, g, hT, faT, gaT, neg_a)
        delta_heads(nc, g, hT, faT, gaT, neg_a)


def low_rank(nc, g, hT, faT, gaT, neg_a):
    with Scope(nc, "low") as sc:
        wfa = sc.sb("wfa", [P, DT, K])
        wga = sc.sb("wga", [P, DT, K])
        wb = sc.sb("wb", [P, DT, HEADS])
        beta = sc.sb("beta", [HEADS, T])
        f_ps = [sc.ps(f"f{c}", [K, S]) for c in range(2)]
        g_ps = [sc.ps(f"g{c}", [K, S]) for c in range(2)]
        b_ps = [sc.ps(f"b{c}", [HEADS, S]) for c in range(2)]
        w_loaded = sc.sem("w_loaded")
        a_loaded = sc.sem("a_loaded")
        a_exp = sc.sem("a_exp")
        f_done = sc.sem("f_done")
        copied = sc.sem("copied")
        beta_done = sc.sem("beta_done")
        beta_stored = sc.sem("beta_stored")
        with nc.Block() as block:
            @block.sync
            def _(sp):
                sp.dma_start(wfa[:], g["kda_wfa"].rearrange("(k p) n -> p k n", p=P)).then_inc(w_loaded, 16)
                sp.dma_start(wga[:], g["kda_wga"].rearrange("(k p) n -> p k n", p=P)).then_inc(w_loaded, 16)
                sp.dma_start(wb[:], g["kda_wb"].rearrange("(k p) n -> p k n", p=P)).then_inc(w_loaded, 16)
                sp.dma_start(neg_a[:], g["kda_a_log"].rearrange("(o n) -> o n", o=1).to_broadcast([P, HEADS])).then_inc(a_loaded, 16)
                sp.wait_ge(beta_done, B)
                sp.dma_start(g["beta_dram"], beta[:]).then_inc(beta_stored, 16)
                sp.wait_ge(w_loaded, 48)
                sp.wait_ge(beta_stored, 16)

            @block.tensor
            def _(pe):
                pe.wait_ge(w_loaded, 48)
                for c in range(B):
                    if c >= 2:
                        pe.wait_ge(copied, 2 * (c - 1))
                        pe.wait_ge(beta_done, c - 1)
                    for w, to in ((wfa, f_ps), (wga, g_ps), (wb, b_ps)):
                        for k in range(DT):
                            last = pe.matmul(to[c % 2][:], w[:, k, :], hT[:, k, c * S:(c + 1) * S],
                                             start=(k == 0), stop=(k == DT - 1))
                    last.then_inc(f_done, 1)

            @block.scalar
            def _(act):
                act.wait_ge(a_loaded, 16)
                act.activation(neg_a[:], neg_a[:], ACT.Exp).then_inc(a_exp, 1)
                for c in range(B):
                    act.wait_ge(f_done, c + 1)
                    act.activation(beta[:, c * S:(c + 1) * S], b_ps[c % 2][:], ACT.Sigmoid).then_inc(beta_done, 1)

            @block.vector
            def _(dve):
                dve.wait_ge(a_exp, 1)
                dve.tensor_scalar(neg_a[:], neg_a[:], -1.0, None, ALU.mult)
                for c in range(B):
                    dve.wait_ge(f_done, c + 1)
                    dve.tensor_copy(faT[:, c * S:(c + 1) * S], f_ps[c % 2][:]).then_inc(copied, 1)
                    dve.tensor_copy(gaT[:, c * S:(c + 1) * S], g_ps[c % 2][:]).then_inc(copied, 1)


def delta_heads(nc, g, hT, faT, gaT, neg_a):
    NL = len(HALVES)
    PAD = TAPS - 1
    N = HEADS * B
    with Scope(nc, "delta_rule") as sc:
        conv_w = [sc.sb(f"conv_w{i}", [P, HEADS, TAPS]) for i in range(3)]
        conv_b = [sc.sb(f"conv_b{i}", [P, HEADS]) for i in range(3)]
        dt_bias = sc.sb("dt_bias", [P, HEADS])
        act_params = sc.sb("act_params", [P, HEADS, 8])
        head_params = sc.sb("head_params", [P, 8])
        o_norm = sc.sb("o_norm", [P, 1])
        eps = sc.sb("eps", [P, 3])
        w_qkv = [sc.sb(f"w{i}", [P, DT, K]) for i in range(3)]
        w_fb = sc.sb("w_fb", [P, K])
        w_gb = sc.sb("w_gb", [P, K])
        w_o = sc.sb("w_o", [P, D])
        beta = [sc.sb(f"beta{j}", [P, S]) for j in range(2)]
        level_mask = sc.sb("level_mask", [P, NL, S // 2], BF16)
        diag_mask = g["ident"][:].unsqueeze(1).to_broadcast([P, CHUNKS, P])
        diag_bits = g["ident"][:].bitcast(U32).unsqueeze(1).to_broadcast([P, CHUNKS, P])
        raw = [sc.sb(f"raw{i}", [P, PAD + S]) for i in range(3)]
        qkv = [[sc.sb(f"qkv{i}_{j}", [P, S]) for i in range(3)] for j in range(2)]
        q_n, k_n, vb = zip(*qkv)
        square = [raw[0][:, PAD:PAD + S], raw[1][:, PAD:PAD + S]]
        inv_norm = [sc.sb(f"inv_norm{i}", [P, S]) for i in range(2)]
        kb = sc.sb("kb", [P, S])
        z = sc.sb("z", [P, S])
        e = sc.sb("e", [P, S])
        u1 = sc.sb("u1", [P, S])
        lnu = sc.sb("lnu", [P, S])
        az = lnu
        prefix = sc.sb("prefix", [P, S])
        suffix = sc.sb("suffix", [P, S])
        k_first = sc.sb("k_first", [P, 2, S])
        qb_second = sc.sb("qb_second", [P, 2, CHUNKS, 2, CHUNK // 2])
        k_state = sc.sb("k_state", [P, S])
        v_rows = [sc.sb(f"v_rows{j}", [P, CHUNKS, K]) for j in range(2)]
        gate = [sc.sb(f"gate{j}", [P, S]) for j in range(2)]
        QT = [sc.sb(f"QT{j}", [P, CHUNKS, CHUNK]) for j in range(2)]
        L_small = [sc.sb(f"L_small{j}", [P, CHUNKS, CHUNK]) for j in range(2)]
        L_large = [sc.sb(f"L_large{j}", [P, CHUNKS, CHUNK]) for j in range(2)]
        kb_state = [sc.sb(f"kb_state{j}", [P, S]) for j in range(2)]
        q_state = [sc.sb(f"q_state{j}", [P, S]) for j in range(2)]
        k_rows = [sc.sb(f"k_rows{j}", [P, CHUNKS, K]) for j in range(2)]
        decay_end = [sc.sb(f"decay_end{j}", [P, CHUNKS]) for j in range(2)]
        X = [sc.sb(f"X{j}", [P, CHUNKS, CHUNK]) for j in range(2)]
        inv = {name: sc.sb(name, [P, CHUNKS, CHUNK]) for name in
               ("LT", "L2", "L2T", "L4", "L4T", "L8T", "WT")}
        inv.update(R=inv["L2"], RT=inv["L2T"], R2=inv["L4"], R2T=inv["L4T"], R4T=inv["LT"])
        state = sc.sb("state", [P, 2, K])
        rhs = sc.sb("rhs", [P, K])
        vd = sc.sb("vd", [P, K])
        o_square = sc.sb("o_square", [P, S])
        o_inv = o_square
        o_gated = sc.sb("o_gated", [P, S])

        proj_ps = [sc.ps(f"proj{i}", [P, CHUNKS, CHUNK]) for i in range(2)]
        level_ps = [sc.ps(f"level{i}", [P, CHUNKS, CHUNK]) for i in range(2)]
        inv_ps = [sc.ps(f"inv{i}", [P, CHUNKS, CHUNK]) for i in range(2)]
        seq_ps = sc.ps("seq", [P, 4, K])
        o_ps = sc.ps("o", [P, S])
        out_ps = [seq_ps[:].rearrange("p a b -> p (a b)"), o_ps[:]]

        params_loaded = sc.sem("params_loaded")
        masks_made = sc.sem("masks_made")
        act_params_made = sc.sem("act_params_made")
        eps_made = sc.sem("eps_made")
        w_loaded = sc.sem("w_loaded")
        wg_loaded = sc.sem("wg_loaded")
        wo_loaded = sc.sem("wo_loaded")
        beta_loaded = [sc.sem(f"beta_loaded{j}") for j in range(2)]
        proj_done = sc.sem("proj_done")
        proj_read = sc.sem("proj_read")
        conv_done = sc.sem("conv_done")
        conv_v_done = sc.sem("conv_v_done")
        silu_done = sc.sem("silu_done")
        silu_v_done = sc.sem("silu_v_done")
        v_projected = sc.sem("v_projected")
        v_read = sc.sem("v_read")
        v_turned = sc.sem("v_turned")
        v_copied = sc.sem("v_copied")
        squared = sc.sem("squared")
        abs_done = sc.sem("abs_done")
        exp_done = sc.sem("exp_done")
        u1_done = sc.sem("u1_done")
        ln_done = sc.sem("ln_done")
        softplus_done = sc.sem("softplus_done")
        decay_done = sc.sem("decay_done")
        inv_norm_done = sc.sem("inv_norm_done")
        vb_done = sc.sem("vb_done")
        q_normed = sc.sem("q_normed")
        k_normed = sc.sem("k_normed")
        k_ready = sc.sem("k_ready")
        qb_ready = sc.sem("qb_ready")
        suffix_done = sc.sem("suffix_done")
        prefix_done = sc.sem("prefix_done")
        level_done = sc.sem("level_done")
        level_read = sc.sem("level_read")
        k_state_done = sc.sem("k_state_done")
        state_ops_done = sc.sem("state_ops_done")
        inv_done = sc.sem("inv_done")
        inv_copied = sc.sem("inv_copied")
        inv_added = sc.sem("inv_added")
        from_state = sc.sem("from_state")
        rhs_done = sc.sem("rhs_done")
        vd_done = sc.sem("vd_done")
        vd_copied = sc.sem("vd_copied")
        to_state = sc.sem("to_state")
        state_done = sc.sem("state_done")
        o_squared = sc.sem("o_squared")
        o_norm_done = sc.sem("o_norm_done")
        o_inv_done = sc.sem("o_inv_done")
        o_ready = sc.sem("o_ready")
        out_done = sc.sem("out_done")
        out_added = sc.sem("out_added")

        SLOTS = 27
        QB_SLOT, LEVEL_SLOT, GATE_SLOT, STATE_SLOT = 11, 12, 21, 26
        CONV_SLOTS, SILU_SLOTS = (1, 2), (1, 3)
        V_PROJ_SLOT, V_OUT_SLOT, CONV_V_SLOTS = 3, 6, (7, 7, 9)
        SILU_V_SLOT, V_BETA_SLOT, V_SLOT = 3, 4, 7
        SQUARE_SLOT, NORM_SLOT, LN_SLOT, EXP_SLOT, GATED_SLOT, OUT_SLOT = 12, 13, 14, 14, 17, 18
        DECAY, Q, KEY, Q_NORM, K_NORM, GATE, K_ROWS, PROJ = range(8)

        COPY_A, COPY_V, ADD, SUB = "scalar copies", "vector copies", "vector adds", "vector subtracts"
        steps = [(2, "LT", "L_small", None, COPY_A, 0, 0),
                 (4, "L2", "LT", "L_small", COPY_A, 1, 0),
                 (4, "L2T", "L_small", "LT", COPY_V, 1, 0),
                 (7, "W", "L2T", "W", ADD, 2, 1),
                 (7, "L4", "L2T", "L2", COPY_A, 2, 1),
                 (7, "L4T", "L2", "L2T", COPY_V, 2, 2),
                 (8, "W", "L4T", "W", ADD, 3, 3),
                 (8, "L8T", "L4", "L4T", COPY_A, 3, 3),
                 (10, "W", "L8T", "W", ADD, 4, 4),
                 (13, "WT", "W", None, COPY_A, 4, 5),
                 (15, "R", "WT", "L_large", COPY_A, 5, 5),
                 (15, "RT", "L_large", "WT", COPY_V, 5, 5),
                 (17, "W", "RT", "W", SUB, 6, 6),
                 (17, "R2", "RT", "R", COPY_A, 6, 6),
                 (17, "R2T", "R", "RT", COPY_V, 6, 7),
                 (19, "W", "R2T", "W", ADD, 7, 8),
                 (19, "R4T", "R2", "R2T", COPY_A, 7, 8),
                 (21, "W", "R4T", "W", ADD, 8, 9)]
        NS = len(steps)
        NC = sum(s[4] == COPY_A for s in steps)
        NV = NS - NC

        def operand(name, p):
            return {"L_small": L_small[p], "L_large": L_large[p], "W": X[p]}.get(name) or inv[name]

        def flat(ap):
            return ap[:].rearrange("p a b -> p (a b)")

        def halves(ap, s, second):
            return ap.rearrange("p (n two s) -> p n two s", two=2, s=s)[:, :, second, :]

        def by_chunk(ap):
            return ap.rearrange("p (c n) s -> p c n s", c=CHUNKS)

        def pipeline(engine, *stages):
            def step(h, b, of):
                for s in range(SLOTS):
                    for d in reversed(of):
                        stages[d](s, h + (b - d) // B, (b - d) % B)

            depth = len(stages)
            for b in range(B):
                step(0, b, [d for d in range(depth) if d <= b])
            with engine.Fori(1, HEADS) as h:
                for b in range(B):
                    step(h, b, range(depth))
            for b in range(depth - 1):
                step(HEADS, b, range(b + 1, depth))

        def first_steps(n):
            return isinstance(n, int) and n < 2

        def bank(i, p):
            return proj_ps[(i + p * PROJ) % 2]

        with nc.Block() as block:
            @block.sync
            def _(sp):
                for i, name in enumerate("qkv"):
                    w, bias = ((g["conv_q_w"], g["conv_q_b"]), (g["conv_k_w"], g["conv_k_b"]), (g["conv_v_w"], g["conv_v_b"]))[i]
                    sp.dma_start(conv_w[i][:], w.rearrange("(h p) j -> p h j", p=P)).then_inc(params_loaded, 16)
                    sp.dma_start(conv_b[i][:], bias).then_inc(params_loaded, 16)
                sp.dma_start(dt_bias[:], g["dt_bias"]).then_inc(params_loaded, 16)
                sp.dma_start(o_norm[:], g["o_norm_w"]).then_inc(params_loaded, 16)

                def load_head(h, later):
                    if later:
                        sp.wait_ge(v_projected, B * h)
                    for w, to in ((g["kda_wq"], w_qkv[0]), (g["kda_wk"], w_qkv[1]), (g["kda_wv"], w_qkv[2])):
                        sp.dma_start(to[:], w.rearrange("(k p) n -> p k n", p=P)[:, :, bass.ds(h * K, K)]).then_inc(w_loaded, 16)
                    sp.dma_start(w_fb[:], g["kda_wfb"][:, bass.ds(h * K, K)]).then_inc(w_loaded, 16)
                    for b in range(B):
                        if later or b > 1:
                            sp.wait_ge(vb_done, h * B + b - 1)
                            sp.wait_ge(k_normed, h * B + b - 1)
                        sp.dma_start(beta[b % 2][:], g["beta_dram"][bass.ds(h, 1), b * S:(b + 1) * S].to_broadcast([P, S])).then_inc(beta_loaded[b % 2], 16)
                        if b == 0:
                            if later:
                                sp.wait_ge(proj_done, PROJ * (B * h - 1) + GATE + 1)
                            sp.dma_start(w_gb[:], g["kda_wgb"][:, bass.ds(h * K, K)]).then_inc(wg_loaded, 16)
                        elif b == 2:
                            if later:
                                sp.wait_ge(out_done, TPB * B * h)
                            sp.dma_start(w_o[:], g["kda_wo"][bass.ds(h * K, K), :]).then_inc(wo_loaded, 16)

                load_head(0, False)
                with sp.Fori(1, HEADS) as h:
                    load_head(h, True)
                sp.wait_ge(params_loaded, 16 * 8)
                sp.wait_ge(w_loaded, 64 * HEADS)
                sp.wait_ge(wg_loaded, 16 * HEADS)
                sp.wait_ge(wo_loaded, 16 * HEADS)
                for j in range(2):
                    sp.wait_ge(beta_loaded[j], 16 * N // 2)

            @block.gpsimd
            def _(pool):
                pool.memset(level_mask[:], 1.0)
                for j in range(2):
                    for buf in (QT[j], L_small[j], L_large[j]):
                        pool.memset(buf[:], 0.0)
                pool.memset(k_first[:], 0.0)
                for i in range(3):
                    pool.memset(raw[i][:], 0.0)
                pool.drain()
                for i, s in enumerate(HALVES):
                    m = level_mask[:, i, :].rearrange("p (c n s) -> p c n s", c=CHUNKS, s=s)
                    pool.affine_select(out=m, in_=m, compare_op=ALU.is_ge, fill=0.0, base=0,
                                       pattern=[[0, CHUNKS], [-2 * s, CHUNK // (2 * s)], [0, s]], channel_multiplier=1)
                    pool.drain()
                    pool.affine_select(out=m, in_=m, compare_op=ALU.is_ge, fill=0.0, base=s - 1,
                                       pattern=[[0, CHUNKS], [2 * s, CHUNK // (2 * s)], [0, s]], channel_multiplier=-1)
                pool.drain()
                pool.nop().then_inc(masks_made, 1)

                def front(slot, h, b):
                    n, p = h * B + b, b % 2
                    if slot == 4:
                        pool.drain()
                        pool.memset(suffix[:], 1.0)
                    elif slot == 6:
                        pool.wait_ge(inv_norm_done, 2 * n + 2)
                        pool.tensor_tensor(q_n[p][:], q_n[p][:], inv_norm[0][:], ALU.mult).then_inc(q_normed, 1)
                    elif LEVEL_SLOT <= slot < LEVEL_SLOT + 2 * NL and (slot - LEVEL_SLOT) % 2 == 0:
                        i = (slot - LEVEL_SLOT) // 2
                        s = HALVES[i]
                        first = halves(suffix[:], s, 0)
                        if i > 0:
                            pool.wait_ge(suffix_done, NL * n + i)
                            if i == 1:
                                pool.wait_ge(k_normed, n + 1)
                            pool.wait_ge(level_done, (NL + 1) * n + i)
                            pool.tensor_tensor(halves(k_first[:, i % 2, :], s, 0), halves(k_n[p][:], s, 0), first,
                                               ALU.mult).then_inc(k_ready, 1)
                            pool.wait_ge(k_ready, (NL - 1) * n + i)
                            pool.wait_ge(prefix_done, NL * n + i)
                        else:
                            pool.drain()
                            pool.wait_ge(decay_done, n + 1)
                        whole_second = halves(prefix[:], s, 1)[:, :, s - 1:s].to_broadcast([P, S // (2 * s), s])
                        pool.tensor_tensor(first, first, whole_second, ALU.mult).then_inc(suffix_done, 1)
                    elif slot == STATE_SLOT:
                        pool.wait_ge(suffix_done, NL * (n + 1))
                        pool.wait_ge(proj_read, PROJ * n)
                        pool.tensor_tensor(k_state[:], k_n[p][:], suffix[:], ALU.mult).then_inc(k_state_done, 1)
                        pool.wait_ge(prefix_done, NL * (n + 1))
                        pool.tensor_tensor(kb_state[p][:], kb[:], prefix[:], ALU.mult)
                        pool.tensor_tensor(q_state[p][:], q_n[p][:], prefix[:], ALU.mult)
                        pool.wait_ge(level_read, (NL + 1) * n + HALVES.index(SMALL))
                        pool.tensor_tensor(X[p][:], diag_mask, L_small[p][:], ALU.subtract).then_inc(state_ops_done, 1)

                def middle(slot, h, b):
                    n, p = h * B + b, b % 2
                    if slot == V_BETA_SLOT:
                        pool.wait_ge(silu_v_done, n + 1)
                        pool.wait_ge(beta_loaded[p], 16 * (h * (B // 2) + b // 2 + 1))
                        pool.tensor_tensor(vb[p][:], vb[p][:], beta[p][:], ALU.mult).then_inc(vb_done, 1)

                def back(slot, h, b):
                    pass

                pipeline(pool, front, middle, back)

            @block.scalar
            def _(act):
                act.wait_ge(params_loaded, 16 * 8)
                act.wait_ge(masks_made, 1)
                act.wait_ge(eps_made, 1)
                act.wait_ge(act_params_made, 1)

                def take_out(i, src, p):
                    act.activation(raw[i][:, PAD:PAD + S], src, ACT.Copy)
                    return act.activation(qkv[p][i][:], src, ACT.Identity, bias=head_params[:, i:i + 1],
                                          scale=head_params[:, 3 + i:4 + i])

                def front(slot, h, b):
                    n, p = h * B + b, b % 2
                    if slot == 0 and b == 0:
                        act.drain()
                        act.activation(head_params[:], act_params[:, h, :], ACT.Copy)
                        act.drain()
                    if slot == 0:
                        act.wait_ge(proj_done, PROJ * n + DECAY + 1)
                        act.activation(z[:], flat(bank(DECAY, p)), ACT.Identity, bias=head_params[:, 6:7]).then_inc(proj_read, 1)
                        act.wait_ge(abs_done, n + 1)
                        act.activation(e[:], az[:], ACT.Exp, scale=-1.0).then_inc(exp_done, 1)
                    if slot in (0, 1):
                        act.wait_ge(proj_done, PROJ * n + Q + slot + 1)
                        take_out(slot, flat(bank(Q + slot, p)), p).then_inc(proj_read, 1)
                    if slot in SILU_SLOTS:
                        i = SILU_SLOTS.index(slot)
                        act.wait_ge(conv_done, 2 * n + i + 1)
                        act.activation(qkv[p][i][:], qkv[p][i][:], ACT.Silu).then_inc(silu_done, 1)
                        act.wait_ge(silu_done, 2 * n + i + 1)
                        act.activation(square[i], qkv[p][i][:], ACT.Square).then_inc(squared, 1)
                    elif slot == 5:
                        act.wait_ge(u1_done, n + 1)
                        act.activation(lnu[:], u1[:], ACT.Ln).then_inc(ln_done, 1)
                        act.wait_ge(proj_done, PROJ * n + Q_NORM + 1)
                        act.activation(inv_norm[0][:], flat(bank(Q_NORM, p)), ACT.Ln, bias=eps[:, 0:1],
                                       scale=float(K)).then_inc(proj_read, 1)
                        act.wait_ge(proj_done, PROJ * n + K_NORM + 1)
                        act.activation(inv_norm[1][:], flat(bank(K_NORM, p)), ACT.Ln, bias=eps[:, 1:2]).then_inc(proj_read, 1)
                    elif slot == 6:
                        act.wait_ge(proj_read, PROJ * n + K_NORM + 1)
                        for i in (1, 0):
                            act.activation(inv_norm[i][:], inv_norm[i][:], ACT.Exp, scale=-0.5).then_inc(inv_norm_done, 1)
                        act.wait_ge(softplus_done, n + 1)
                        act.activation(prefix[:], lnu[:], ACT.Exp, scale=head_params[:, 7:8]).then_inc(decay_done, 1)
                    elif slot == GATE_SLOT:
                        act.wait_ge(proj_done, PROJ * n + GATE + 1)
                        if not first_steps(n):
                            act.wait_ge(o_ready, n - 1)
                        act.activation(gate[p][:], flat(bank(GATE, p)), ACT.Sigmoid).then_inc(proj_read, 1)

                    if slot == V_OUT_SLOT:
                        act.wait_ge(v_projected, n + 1)
                        take_out(2, flat(level_ps[0]), p).then_inc(v_read, 1)

                def middle(slot, h, b):
                    n, p = h * B + b, b % 2
                    if slot == 0:
                        act.wait_ge(proj_done, PROJ * n + K_ROWS + 1)
                        act.activation(k_rows[p][:], bank(K_ROWS, p)[:], ACT.Copy).then_inc(proj_read, 1)
                    elif slot == SILU_V_SLOT:
                        act.wait_ge(conv_v_done, n + 1)
                        act.activation(vb[p][:], vb[p][:], ACT.Silu).then_inc(silu_v_done, 1)
                    elif slot == V_SLOT:
                        if not first_steps(n):
                            act.wait_ge(to_state, CHUNKS * (n - 1))
                        act.wait_ge(v_turned, n + 1)
                        act.activation(v_rows[p][:], level_ps[1][:], ACT.Copy).then_inc(v_copied, 1)
                    for i, (at, name, left, right, by, _, _) in enumerate(steps):
                        if at == slot and by == COPY_A:
                            act.wait_ge(inv_done, NS * n + i + 1)
                            act.activation(inv[name][:], inv_ps[i % 2][:], ACT.Copy).then_inc(inv_copied, 1)

                def back(slot, h, b):
                    n = h * B + b
                    if slot < 3 * CHUNKS and slot % 3 == 1:
                        c = slot // 3
                        act.wait_ge(vd_done, CHUNKS * n + c + 1)
                        act.wait_ge(to_state, CHUNKS * n + c)
                        act.activation(vd[:], seq_ps[:, 1, :], ACT.Copy).then_inc(vd_copied, 1)
                    elif slot == SQUARE_SLOT:
                        act.wait_ge(to_state, CHUNKS * (n + 1))
                        act.wait_ge(o_ready, n)
                        act.activation(o_square[:], o_ps[:], ACT.Square).then_inc(o_squared, 1)
                    elif slot == LN_SLOT:
                        act.wait_ge(o_norm_done, n + 1)
                        act.activation(o_inv[:], flat(seq_ps), ACT.Ln, bias=eps[:, 2:3], scale=1.0 / K)
                    if slot == EXP_SLOT:
                        act.drain()
                        act.activation(o_inv[:], o_inv[:], ACT.Exp, scale=-0.5).then_inc(o_inv_done, 1)

                pipeline(act, front, middle, back)

            @block.vector
            def _(dve):
                for i, value in enumerate((L2_EPS * K, L2_EPS, O_EPS)):
                    last = dve.memset(eps[:, i:i + 1], value)
                last.then_inc(eps_made, 1)
                dve.wait_ge(params_loaded, 16 * 8)
                for i in range(3):
                    dve.tensor_copy(act_params[:, :, i], conv_b[i][:])
                    dve.tensor_copy(act_params[:, :, 3 + i], conv_w[i][:, :, PAD])
                dve.tensor_copy(act_params[:, :, 6], dt_bias[:])
                dve.tensor_copy(act_params[:, :, 7], neg_a[:]).then_inc(act_params_made, 1)
                dve.wait_ge(masks_made, 1)

                def front(slot, h, b):
                    n, p = h * B + b, b % 2

                    def take(i):
                        s = HALVES[i]
                        mask = by_chunk(level_mask[:, i, :].bitcast(U16).rearrange("p (n s) -> p n s", s=s))
                        for j, to in enumerate((QT[p], L_small[p] if s < SMALL else L_large[p])):
                            data = level_ps[(i + 1) % 2][:].rearrange("p c (j m) -> p c j m", j=2)[:, :, j, :]
                            last = dve.copy_predicated(by_chunk(halves(flat(to), s, 1)), mask,
                                                       data.rearrange("p c (n s) -> p c n s", s=s))
                        last.then_inc(level_read, 1)

                    def second_halves(i):
                        s = HALVES[i]
                        for j, src in enumerate((q_n[p], kb)):
                            last = dve.tensor_tensor(qb_second[:, i % 2, :, j, :].rearrange("p c (n s) -> p c n s", s=s),
                                                     by_chunk(halves(src[:], s, 1)), by_chunk(halves(prefix[:], s, 1)), ALU.mult)
                        last.then_inc(qb_ready, 1)

                    def conv_tap(i, back_by):
                        return dve.scalar_tensor_tensor(qkv[p][i][:], raw[i][:, PAD - back_by:PAD - back_by + S],
                                                        conv_w[i][:, h, PAD - back_by:PAD - back_by + 1], qkv[p][i][:],
                                                        ALU.mult, ALU.add)

                    if slot == 0:
                        dve.wait_ge(proj_read, PROJ * n + DECAY + 1)
                        dve.scalar_tensor_tensor(az[:], z[:], -1.0, z[:], ALU.mult, ALU.max).then_inc(abs_done, 1)
                        dve.wait_ge(exp_done, n + 1)
                        dve.tensor_scalar(u1[:], e[:], 1.0, None, ALU.add).then_inc(u1_done, 1)
                        dve.drain()
                        dve.scalar_tensor_tensor(e[:], u1[:], 1.0, e[:], ALU.subtract, ALU.subtract)
                    elif slot in CONV_SLOTS:
                        i = CONV_SLOTS.index(slot)
                        dve.wait_ge(proj_read, PROJ * n + Q + i + 1)
                        for back_by in range(1, TAPS):
                            last = conv_tap(i, back_by)
                            if back_by < TAPS - 1:
                                dve.drain()
                        last.then_inc(conv_done, 1)
                    elif slot == 6:
                        dve.wait_ge(ln_done, n + 1)
                        dve.scalar_tensor_tensor(lnu[:], u1[:], 1.0, lnu[:], ALU.is_gt, ALU.mult)
                        dve.drain()
                        dve.tensor_tensor(lnu[:], lnu[:], e[:], ALU.subtract)
                        dve.drain()
                        dve.scalar_tensor_tensor(lnu[:], z[:], 0.0, lnu[:], ALU.max, ALU.add).then_inc(softplus_done, 1)
                        dve.wait_ge(inv_norm_done, 2 * n + 1)
                        dve.tensor_tensor(k_n[p][:], k_n[p][:], inv_norm[1][:], ALU.mult)
                        dve.drain()
                        dve.wait_ge(beta_loaded[p], 16 * (h * (B // 2) + b // 2 + 1))
                        dve.tensor_tensor(kb[:], k_n[p][:], beta[p][:], ALU.mult).then_inc(k_normed, 1)
                    elif slot == QB_SLOT:
                        dve.drain()
                        dve.wait_ge(decay_done, n + 1)
                        dve.wait_ge(q_normed, n + 1)
                        second_halves(0)
                    elif LEVEL_SLOT <= slot < LEVEL_SLOT + 2 * NL and (slot - LEVEL_SLOT) % 2 == 0:
                        i = (slot - LEVEL_SLOT) // 2
                        whole_first = halves(prefix[:], HALVES[i], 0)[:, :, HALVES[i] - 1:HALVES[i]].to_broadcast([P, S // (2 * HALVES[i]), HALVES[i]])
                        dve.wait_ge(suffix_done, NL * n + i + 1)
                        dve.wait_ge(level_done, (NL + 1) * n + i + 1)
                        if i == 0 and not first_steps(n):
                            dve.wait_ge(to_state, CHUNKS * (n - 1))
                        dve.tensor_tensor(halves(prefix[:], HALVES[i], 1), halves(prefix[:], HALVES[i], 1), whole_first, ALU.mult).then_inc(prefix_done, 1)
                        dve.drain()
                        if i + 1 < NL:
                            second_halves(i + 1)
                        if i == 0:
                            dve.copy_predicated(QT[p][:], diag_bits, level_ps[0][:]).then_inc(level_read, 1)
                        else:
                            take(i - 1)
                    elif slot == STATE_SLOT:
                        dve.drain()
                        dve.wait_ge(level_done, (NL + 1) * (n + 1))
                        dve.tensor_copy(decay_end[p][:], prefix[:].rearrange("p (c t) -> p c t", c=CHUNKS)[:, :, CHUNK - 1])
                        take(NL - 1)
                    for back_by in range(1, TAPS):
                        if slot == CONV_V_SLOTS[back_by - 1]:
                            if back_by == 1:
                                dve.wait_ge(v_read, n + 1)
                            else:
                                dve.drain()
                            last = conv_tap(2, back_by)
                            if back_by == TAPS - 1:
                                last.then_inc(conv_v_done, 1)

                def middle(slot, h, b):
                    n, p = h * B + b, b % 2
                    for i, (at, name, left, right, by, _, _) in enumerate(steps):
                        if at == slot and by != COPY_A:
                            dve.wait_ge(inv_done, NS * n + i + 1)
                            if by == COPY_V:
                                dve.tensor_copy(inv[name][:], inv_ps[i % 2][:]).then_inc(inv_added, 1)
                            else:
                                dve.tensor_tensor(X[p][:], X[p][:], inv_ps[i % 2][:],
                                                  ALU.add if by == ADD else ALU.subtract).then_inc(inv_added, 1)

                def back(slot, h, b):
                    n, p = h * B + b, b % 2
                    if slot < 3 * CHUNKS:
                        c, part = divmod(slot, 3)
                        if part == 0 and c > 0:
                            dve.wait_ge(from_state, (CHUNKS - 1) * n + c)
                            dve.tensor_tensor(rhs[:], v_rows[p][:, c, :], seq_ps[:, 0, :], ALU.subtract).then_inc(rhs_done, 1)
                        elif part == 2 and c < CHUNKS - 1:
                            dve.drain()
                            dve.wait_ge(to_state, CHUNKS * n + c + 1)
                            if c == 0:
                                dve.tensor_copy(state[:, 0, :], seq_ps[:, 2, :]).then_inc(state_done, 1)
                            else:
                                dve.scalar_tensor_tensor(state[:, c % 2, :], state[:, (c + 1) % 2, :], decay_end[p][:, c:c + 1],
                                                         seq_ps[:, 2, :], ALU.mult, ALU.add).then_inc(state_done, 1)
                    elif slot == GATED_SLOT:
                        dve.drain()
                        dve.wait_ge(o_norm_done, n + 1)
                        dve.scalar_tensor_tensor(o_gated[:], o_ps[:], o_norm[:], gate[p][:], ALU.mult, ALU.mult)
                        dve.drain()
                        dve.wait_ge(o_inv_done, n + 1)
                        dve.tensor_tensor(o_gated[:], o_gated[:], o_inv[:], ALU.mult).then_inc(o_ready, 1)
                    elif slot > OUT_SLOT and (slot - OUT_SLOT) % 2 == 1 and slot < OUT_SLOT + 2 * TPB:
                        t = (slot - OUT_SLOT) // 2
                        xr = g["x"][:, b * TPB + t, :]
                        dve.wait_ge(out_done, TPB * n + t + 1)
                        dve.tensor_tensor(xr, xr, out_ps[t % 2], ALU.add).then_inc(out_added, 1)

                pipeline(dve, front, middle, back)

            @block.tensor
            def _(pe):
                pe.wait_ge(masks_made, 1)

                def free_bank(i, n, p):
                    before = PROJ * n + i - 1
                    if not (first_steps(n) and before <= 0):
                        pe.wait_ge(proj_read, before)
                    return bank(i, p)

                def front(slot, h, b):
                    n, p = h * B + b, b % 2
                    tokens = slice(b * S, (b + 1) * S)

                    if slot in (0, 1, V_PROJ_SLOT):
                        if slot == 0:
                            pe.wait_ge(w_loaded, 64 * (h + 1))
                            pe.matmul(flat(free_bank(DECAY, n, p)), w_fb[:], faT[:, tokens], start=True, stop=True).then_inc(proj_done, 1)
                        i = min(slot, 2)
                        if i == 2:
                            pe.wait_ge(level_read, (NL + 1) * n)
                        to = flat(level_ps[0] if i == 2 else free_bank(Q + i, n, p))
                        for k in range(DT):
                            last = pe.matmul(to, w_qkv[i][:, k, :], hT[:, k, tokens], start=(k == 0), stop=(k == DT - 1))
                        last.then_inc(v_projected if i == 2 else proj_done, 1)
                    if slot == 5:
                        for i in range(2):
                            pe.wait_ge(squared, 2 * n + i + 1)
                            pe.matmul(flat(free_bank(Q_NORM + i, n, p)), g["ones"][:], square[i], start=True, stop=True).then_inc(proj_done, 1)
                    if slot == GATE_SLOT:
                        pe.wait_ge(wg_loaded, 16 * (h + 1))
                        pe.matmul(flat(free_bank(GATE, n, p)), w_gb[:], gaT[:, tokens], start=True, stop=True).then_inc(proj_done, 1)
                    if slot == LEVEL_SLOT:
                        pe.wait_ge(q_normed, n + 1)
                        pe.wait_ge(k_normed, n + 1)
                        pe.wait_ge(v_read, n + 1)
                        for c in range(CHUNKS):
                            at = slice(c * CHUNK, (c + 1) * CHUNK)
                            last = pe.matmul(level_ps[0][:, c, :], k_n[p][:, at], q_n[p][:, at], start=True, stop=True)
                        last.then_inc(level_done, 1)
                    if LEVEL_SLOT <= slot < LEVEL_SLOT + 2 * NL and (slot - LEVEL_SLOT) % 2 == 0:
                        i = (slot - LEVEL_SLOT) // 2
                        pe.wait_ge(qb_ready, NL * n + i + 1)
                        pe.wait_ge(k_ready, (NL - 1) * n + i)
                        pe.wait_ge(level_read, (NL + 1) * n + i)
                        if i == 0:
                            pe.wait_ge(v_copied, n)
                        for c in range(CHUNKS):
                            at = slice(c * CHUNK, (c + 1) * CHUNK)
                            left = k_n[p][:, at] if i == 0 else k_first[:, i % 2, at]
                            last = pe.matmul(level_ps[(i + 1) % 2][:, c, :], left,
                                             qb_second[:, i % 2, c, :, :].rearrange("p j m -> p (j m)"), start=True, stop=True)
                        last.then_inc(level_done, 1)

                def middle(slot, h, b):
                    n, p = h * B + b, b % 2
                    if slot == 0:
                        pe.wait_ge(k_state_done, n + 1)
                        to = free_bank(K_ROWS, n, p)
                        for c in range(CHUNKS):
                            last = pe.transpose(to[:, c, :], k_state[:, c * CHUNK:(c + 1) * CHUNK], g["ident"][:])
                        last.then_inc(proj_done, 1)
                    elif slot == V_SLOT:
                        pe.wait_ge(vb_done, n + 1)
                        pe.wait_ge(level_read, (NL + 1) * (n + 1))
                        for c in range(CHUNKS):
                            last = pe.transpose(level_ps[1][:, c, :], vb[p][:, c * CHUNK:(c + 1) * CHUNK], g["ident"][:])
                        last.then_inc(v_turned, 1)
                    for i, (at, name, left, right, by, copied, added) in enumerate(steps):
                        if at == slot:
                            if i == 0:
                                pe.wait_ge(state_ops_done, n + 1)
                                pe.wait_ge(level_read, (NL + 1) * (n + 1))
                            pe.wait_ge(inv_copied, NC * n + copied)
                            pe.wait_ge(inv_added, NV * n + added)
                            for c in range(CHUNKS):
                                if right is None:
                                    last = pe.transpose(inv_ps[i % 2][:, c, :], operand(left, p)[:, c, :], g["ident"][:])
                                else:
                                    last = pe.matmul(inv_ps[i % 2][:, c, :], operand(left, p)[:, c, :], operand(right, p)[:, c, :],
                                                     start=True, stop=True)
                            last.then_inc(inv_done, 1)

                def back(slot, h, b):
                    n, p = h * B + b, b % 2
                    if slot < 3 * CHUNKS:
                        c, part = divmod(slot, 3)
                        at = slice(c * CHUNK, (c + 1) * CHUNK)
                        last_state = state[:, (c + 1) % 2, :]
                        if part == 0 and c > 0:
                            pe.wait_ge(state_done, (CHUNKS - 1) * n + c)
                            pe.matmul(seq_ps[:, 0, :], kb_state[p][:, at], last_state, start=True, stop=True).then_inc(from_state, 1)
                        elif part == 1:
                            if c == 0:
                                pe.wait_ge(inv_added, NV * (n + 1))
                                pe.wait_ge(out_added, TPB * n)
                            pe.wait_ge(rhs_done, (CHUNKS - 1) * n + c)
                            pe.matmul(seq_ps[:, 1, :], X[p][:, c, :], v_rows[p][:, c, :] if c == 0 else rhs[:],
                                      start=True, stop=True).then_inc(vd_done, 1)
                        elif part == 2:
                            pe.wait_ge(vd_copied, CHUNKS * n + c + 1)
                            pe.matmul(seq_ps[:, 2, :], k_rows[p][:, c, :], vd[:], start=True, stop=True)
                            if c > 0:
                                pe.matmul(o_ps[:, at], last_state, q_state[p][:, at], start=True, stop=False)
                            pe.matmul(o_ps[:, at], vd[:], QT[p][:, c, :], start=(c == 0), stop=True).then_inc(to_state, 1)
                    elif slot == NORM_SLOT:
                        pe.wait_ge(o_squared, n + 1)
                        pe.wait_ge(state_done, (CHUNKS - 1) * (n + 1))
                        pe.matmul(flat(seq_ps), g["ones"][:], o_square[:], start=True, stop=True).then_inc(o_norm_done, 1)
                    elif OUT_SLOT <= slot < OUT_SLOT + 2 * TPB and (slot - OUT_SLOT) % 2 == 0:
                        t = (slot - OUT_SLOT) // 2
                        if t == 0:
                            pe.wait_ge(o_ready, n + 1)
                            pe.wait_ge(wo_loaded, 16 * (h + 1))
                        else:
                            pe.wait_ge(out_added, TPB * n + max(t - 1, 0))
                        pe.matmul(out_ps[t % 2], o_gated[:, t * P:(t + 1) * P], w_o[:], start=True, stop=True).then_inc(out_done, 1)

                pipeline(pe, front, middle, back)



X_HEADS, X_DIM, CTX_DIM = 32, 16, 256
AXES, HALF = 2, 4
ANGLES = AXES * HALF
PARTS = 3
PART_PAIRS = [(a, b) for a in range(PARTS) for b in range(PARTS) if a + b < 2 * PARTS - 2]
FREQUENCIES = [10000.0 ** (-i / HALF) for i in range(HALF)]
HEADS_PER_TILE = P // X_DIM
CT = CTX_DIM // P
TWO_PI = 6.283185307179586
TURN = [6.28125, 0.0019350051879882812, 3.019916050561733e-07]
HALF_PI, PI_BELOW = 1.5707963267948966, 3.1415925


def cross_attention_layer(nc, g):
    with Scope(nc, "xattn") as outer:
        v_tiles = outer.sb("v_tiles", [P, B, DT, TPB, P])
        with Scope(nc, "xattn_q") as inner:
            hT = inner.sb("hT", [P, DT, T])
            layer_norm(nc, g, "xattn", hT)
            cos = inner.sb("cos", [P, NT, ANGLES])
            sin = inner.sb("sin", [P, NT, ANGLES])
            rotary_tables(nc, g, cos, sin)
            project_qkv(nc, g, hT, v_tiles, cos, sin)
        attended = outer.sb("attended", [P, B, DT, S])
        sums = outer.sb("sums", [P, B, DT, HEADS_PER_TILE, TPB])
        attend(nc, g, v_tiles, attended, sums)
        project_attended(nc, g, attended, sums)


def rotary_tables(nc, g, cos, sin):
    with Scope(nc, "tables") as sc:
        pos = sc.sb("pos", [P, NT, AXES])
        angle = sc.sb("angle", [P, NT, AXES, HALF])
        turns = sc.sb("turns", [P, NT, AXES, HALF])
        quarter = sc.sb("quarter", [P, NT, AXES, HALF])
        pos_loaded = sc.sem("pos_loaded")
        reduced = sc.sem("reduced")
        with nc.Block() as block:
            @block.sync
            def _(sp):
                sp.dma_start(pos[:], g["pos"].rearrange("(t p) a -> p t a", p=P)).then_inc(pos_loaded, 16)
                sp.wait_ge(pos_loaded, 16)

            @block.vector
            def _(dve):
                dve.wait_ge(pos_loaded, 16)
                for f, freq in enumerate(FREQUENCIES):
                    dve.tensor_scalar(angle[:, :, :, f], pos[:], freq, None, ALU.mult)
                dve.drain()
                dve.tensor_scalar(turns[:], angle[:], 1.0 / TWO_PI, ROUND, ALU.mult, ALU.add)
                dve.drain()
                dve.tensor_scalar(turns[:], turns[:], ROUND, None, ALU.subtract)
                for part in TURN:
                    dve.drain()
                    dve.scalar_tensor_tensor(angle[:], turns[:], -part, angle[:], ALU.mult, ALU.add)
                dve.drain()
                dve.tensor_scalar(angle[:], angle[:], PI_BELOW, -PI_BELOW, ALU.min, ALU.max)
                dve.drain()
                dve.scalar_tensor_tensor(quarter[:], angle[:], -1.0, angle[:], ALU.mult, ALU.max)
                dve.drain()
                dve.tensor_scalar(quarter[:], quarter[:], -1.0, HALF_PI, ALU.mult, ALU.add).then_inc(reduced, 1)

            @block.scalar
            def _(act):
                act.wait_ge(reduced, 1)
                act.activation(cos[:], quarter[:].rearrange("p t a f -> p t (a f)"), ACT.Sin)
                act.activation(sin[:], angle[:].rearrange("p t a f -> p t (a f)"), ACT.Sin)


def project_qkv(nc, g, hT, v_tiles, cos, sin):
    BODY = 2 * TPB
    with Scope(nc, "qkv") as sc:
        wq = sc.sb("wq", [P, DT, D])
        wkv = sc.sb("wkv", [P, CT, 2 * D])
        h_tile = sc.sb("h_tile", [P, 2, DT, P])
        ctx_tile = sc.sb("ctx_tile", [P, 2, CT, P])
        products = sc.sb("products", [P, 2, 4, D // 2])
        rotated = sc.sb("rotated", [P, 2, D])
        rest = sc.sb("rest", [P, 2, DT, P])
        parts = sc.sb("parts", [P, 2, 2, PARTS, DT, S], BF16)
        q_ps = [sc.ps(f"q_ps{j}", [P, D]) for j in range(2)]
        k_ps = [sc.ps(f"k_ps{j}", [P, D]) for j in range(2)]
        v_ps = [sc.ps(f"v_ps{j}", [P, DT, P]) for j in range(2)]
        turned_ps = [sc.ps(f"turned{i}", [P, DT, P]) for i in range(2)]
        w_loaded = sc.sem("w_loaded")
        ctx_loaded = [sc.sem(f"ctx_loaded{j}") for j in range(2)]
        h_copied = sc.sem("h_copied")
        qkv_done = sc.sem("qkv_done")
        v_copied = sc.sem("v_copied")
        rotated_done = sc.sem("rotated_done")
        turned = sc.sem("turned")
        first_done = sc.sem("first_done")
        rest_done = sc.sem("rest_done")
        second_done = sc.sem("second_done")
        parts_done = sc.sem("parts_done")
        parts_stored = sc.sem("parts_stored")
        SCALES = (float(X_DIM) ** -0.5, 1.0)
        with nc.Block() as block:
            @block.sync
            def _(sp):
                sp.sem_inc(qkv_done, 2)
                sp.sem_inc(v_copied, 2)
                sp.sem_inc(rotated_done, 4)
                sp.dma_start(wq[:], g["wq"].rearrange("(k p) n -> p k n", p=P)).then_inc(w_loaded, 16)
                sp.dma_start(wkv[:], g["wkv"].rearrange("(k p) n -> p k n", p=P)).then_inc(w_loaded, 16)
                with sp.Fori(0, B // 2) as bb:
                    for half in range(2):
                        for i in range(TPB):
                            sp.wait_ge(qkv_done, bb * BODY + half * TPB + i + 1)
                            sp.dma_start(ctx_tile[:, i % 2, :, :], g["ctx_T"][2 * bb + half].rearrange("(k p) t -> p k t", p=P)[
                                :, :, i * P:(i + 1) * P]).then_inc(ctx_loaded[i % 2], 16)
                sp.wait_ge(w_loaded, 32)
                for j in range(2):
                    sp.wait_ge(ctx_loaded[j], 16 * NT // 2)

            @block.gpsimd
            def _(pool):
                with pool.Fori(0, B // 2) as bb:
                    for half in range(2):
                        for i in range(TPB):
                            for w in range(2):
                                n = 2 * (bb * BODY + half * TPB + i) + w
                                at = slice(i * P, (i + 1) * P)
                                pool.wait_ge(rest_done, n + 1)
                                pool.tensor_tensor(parts[:, half, w, 1, :, at], rest[:, w, :, :],
                                                   g["ones"][:].unsqueeze(1).to_broadcast([P, DT, P]), ALU.mult).then_inc(second_done, 1)
                                pool.wait_ge(second_done, n + 1)
                                pool.tensor_tensor(parts[:, half, w, 2, :, at], rest[:, w, :, :], parts[:, half, w, 1, :, at],
                                                   ALU.subtract).then_inc(parts_done, 1)
                        pool.wait_ge(parts_done, 2 * (bb * BODY + (half + 1) * TPB))
                        for w in range(2):
                            for part in range(PARTS):
                                pool.dma_start(g["parts_dram"][w, part, bass.ds(2 * bb + half, 1)].rearrange("o c p s -> p (o c) s"),
                                               parts[:, half, w, part, :, :]).then_inc(parts_stored, 16)
                pool.wait_ge(parts_stored, 16 * 2 * PARTS * B)

            @block.scalar
            def _(act):
                with act.Fori(0, B // 2) as bb:
                    def copy_h(i):
                        t = bb * BODY + i
                        act.wait_ge(qkv_done, t + 1)
                        act.activation(h_tile[:, i % 2, :, :], hT[:, :, bass.ds(t * P, P)], ACT.Copy).then_inc(h_copied, 1)

                    copy_h(0)
                    for i in range(BODY):
                        t = bb * BODY + i
                        half, at = i // TPB, slice(i % TPB * P, (i % TPB + 1) * P)
                        if i + 1 < BODY:
                            copy_h(i + 1)
                        act.wait_ge(qkv_done, 2 + t + 1)
                        act.activation(v_tiles[:, bass.ds(2 * bb + half, 1), :, i % TPB, :].rearrange("p o c d -> p (o c) d"),
                                       v_ps[i % 2][:], ACT.Copy).then_inc(v_copied, 1)
                        for w in range(2):
                            act.wait_ge(turned, 2 * t + w + 1)
                            act.wait_ge(parts_stored, 16 * 2 * PARTS * (2 * bb + half - 1 if half else 2 * bb))
                            act.activation(parts[:, half, w, 0, :, at], turned_ps[w][:], ACT.Copy, scale=SCALES[w]).then_inc(first_done, 1)

            @block.tensor
            def _(pe):
                pe.wait_ge(w_loaded, 32)
                with pe.Fori(0, B // 2) as bb:
                    def project(i):
                        t, j = bb * BODY + i, i % 2
                        pe.wait_ge(h_copied, t + 1)
                        pe.wait_ge(ctx_loaded[j], 16 * (bb * BODY // 2 + i // 2 + 1))
                        pe.wait_ge(v_copied, t + 1)
                        pe.wait_ge(rotated_done, 2 * t + 2)
                        for k in range(DT):
                            pe.matmul(q_ps[j][:], h_tile[:, j, k, :], wq[:, k, :], start=(k == 0), stop=(k == DT - 1))
                        for to, lo in ((k_ps[j][:], 0), (v_ps[j][:].rearrange("p c d -> p (c d)"), D)):
                            for k in range(CT):
                                last = pe.matmul(to, ctx_tile[:, j, k, :], wkv[:, k, lo:lo + D],
                                                 start=(k == 0), stop=(k == CT - 1))
                        last.then_inc(qkv_done, 1)

                    project(0)
                    for i in range(BODY):
                        if i + 1 < BODY:
                            project(i + 1)
                        for w in range(2):
                            n = 2 * (bb * BODY + i) + w
                            pe.wait_ge(rotated_done, 4 + n + 1)
                            pe.wait_ge(rest_done, 2 * (bb * BODY + i))
                            for k in range(DT):
                                last = pe.transpose(turned_ps[w][:, k, :], rotated[:, w, k * P:(k + 1) * P], g["ident"][:])
                            last.then_inc(turned, 1)

            @block.vector
            def _(dve):
                with dve.Fori(0, B // 2) as bb:
                    def rotate(i, w):
                        t = bb * BODY + i
                        src = (q_ps, k_ps)[w][i % 2]
                        shape = [P, X_HEADS, ANGLES]
                        pairs = src[:].rearrange("p (h f two) -> p h f two", h=X_HEADS, two=2)
                        outs = rotated[:, w, :].rearrange("p (h f two) -> p h f two", h=X_HEADS, two=2)
                        prod = [products[:, w, a, :].rearrange("p (h f) -> p h f", h=X_HEADS) for a in range(4)]
                        c = cos[:, bass.ds(t, 1), :].to_broadcast(shape)
                        s = sin[:, bass.ds(t, 1), :].to_broadcast(shape)
                        dve.wait_ge(qkv_done, 2 + t + 1)
                        dve.tensor_tensor(prod[0], pairs[:, :, :, 0], c, ALU.mult)
                        dve.tensor_tensor(prod[1], pairs[:, :, :, 1], s, ALU.mult)
                        dve.tensor_tensor(prod[2], pairs[:, :, :, 0], s, ALU.mult)
                        dve.tensor_tensor(prod[3], pairs[:, :, :, 1], c, ALU.mult)
                        dve.drain()
                        dve.wait_ge(turned, 2 * t)
                        dve.tensor_tensor(outs[:, :, :, 0], prod[0], prod[1], ALU.subtract)
                        dve.tensor_tensor(outs[:, :, :, 1], prod[2], prod[3], ALU.add).then_inc(rotated_done, 1)

                    def split(i, w):
                        n = 2 * (bb * BODY + i) + w
                        at = slice(i % TPB * P, (i % TPB + 1) * P)
                        dve.wait_ge(first_done, n + 1)
                        dve.wait_ge(parts_done, 2 * (bb * BODY + i))
                        dve.scalar_tensor_tensor(rest[:, w, :, :], turned_ps[w][:], SCALES[w], parts[:, i // TPB, w, 0, :, at],
                                                 ALU.mult, ALU.subtract).then_inc(rest_done, 1)

                    for i in range(BODY):
                        for w in range(2):
                            rotate(i, w)
                        if i > 0:
                            for w in range(2):
                                split(i - 1, w)
                    for w in range(2):
                        split(BODY - 1, w)
                    dve.drain()


def attend(nc, g, v_tiles, attended, sums):
    H = HEADS_PER_TILE
    N = B * DT
    RING = 4
    with Scope(nc, "attend") as sc:
        bout = sc.sb("bout", [P, D])
        q_stack = sc.sb("q_stack", [P, RING, S], BF16)
        k_stack = sc.sb("k_stack", [P, RING, S], BF16)
        v_head = sc.sb("v_head", [P, H, TPB, P])
        top = sc.sb("top", [P, 2, TPB])
        head_sums = sc.sb("head_sums", [P, 2, TPB])
        probs = sc.sb("probs", [P, 2, TPB, S])
        probsT = sc.sb("probsT", [P, 2, TPB, S])
        scores = [sc.ps(f"scores{i}", [P, S]) for i in range(TPB)]
        turned = [sc.ps(f"turned{j}", [P, TPB, P]) for j in range(2)]
        out_ps = sc.ps("out_ps", [P, S])
        bout_loaded = sc.sem("bout_loaded")
        stack_loaded = [sc.sem(f"stack_loaded{s}") for s in range(RING)]
        v_ready = sc.sem("v_ready")
        scores_done = sc.sem("scores_done")
        max_done = sc.sem("max_done")
        exp_done = sc.sem("exp_done")
        sums_copied = sc.sem("sums_copied")
        probs_turned = sc.sem("probs_turned")
        even_copied = sc.sem("even_copied")
        odd_copied = sc.sem("odd_copied")
        weighed = sc.sem("weighed")
        out_copied = sc.sem("out_copied")
        v_flat = v_tiles[:].rearrange("p b c i d -> p (b c) i d")
        out_flat = attended[:].rearrange("p b c s -> p (b c) s")
        sums_flat = sums[:].rearrange("p b c h i -> p (b c) h i")
        q_dram = g["parts_dram"][0].rearrange("e b c p s -> e (b c) p s")
        k_dram = g["parts_dram"][1].rearrange("e b c p s -> e (b c) p s")

        def steps(engine, step):
            for j in range(H):
                step(0, j, j == 0, False)
            with engine.Fori(1, N - 1) as n:
                for j in range(H):
                    step(n, j, False, False)
            for j in range(H):
                step(N - 1, j, False, j == H - 1)

        with nc.Block() as block:
            @block.sync
            def _(sp):
                sp.sem_inc(scores_done, RING * TPB)
                sp.sem_inc(exp_done, TPB)
                sp.sem_inc(weighed, H)
                sp.sem_inc(sums_copied, 2)
                sp.dma_start(bout[:], g["bout"].rearrange("(o n) -> o n", o=1).to_broadcast([P, D])).then_inc(bout_loaded, 16)
                with sp.Fori(0, N) as n:
                    for j in range(H):
                        s = j % RING
                        at = slice(j * X_DIM, (j + 1) * X_DIM)
                        sp.wait_ge(scores_done, TPB * (n * H + j + 1))
                        for a in range(PARTS):
                            pairs = [pair for pair in PART_PAIRS if pair[0] == a]
                            lo, count = PART_PAIRS.index(pairs[0]) * X_DIM, len(pairs)
                            to = slice(lo, lo + count * X_DIM)
                            sp.dma_start(q_stack[to, s, :], q_dram[a, bass.ds(n, 1), at, :].to_broadcast(
                                [count, X_DIM, S])).then_inc(stack_loaded[s], 16)
                            sp.dma_start(k_stack[to, s, :], k_dram[0:count, bass.ds(n, 1), at, :].rearrange(
                                "e o d s -> (e o) d s")).then_inc(stack_loaded[s], 16)
                sp.wait_ge(bout_loaded, 16)
                for s in range(RING):
                    sp.wait_ge(stack_loaded[s], 16 * 2 * PARTS * N * H // RING)

            @block.gpsimd
            def _(pool):
                pool.memset(v_head[:], 0.0)
                pool.drain()
                with pool.Fori(0, N) as n:
                    for j in range(H):
                        at = slice(j * X_DIM, (j + 1) * X_DIM)
                        pool.wait_ge(weighed, n * H + j + 1)
                        pool.tensor_copy(v_head[:, j, :, at], v_flat[:, n, :, at]).then_inc(v_ready, 1)
                pool.wait_ge(bout_loaded, 16)
                for t in range(NT):
                    pool.tensor_tensor(g["x"][:, t, :], g["x"][:, t, :], bout[:], ALU.add)

            @block.tensor
            def _(pe):
                def score(n, j):
                    m, s = n * H + j, j % RING
                    pe.wait_ge(stack_loaded[s], 16 * 2 * PARTS * (n * (H // RING) + j // RING + 1))
                    for i in range(TPB):
                        pe.wait_ge(exp_done, TPB * m + i + 1)
                        pe.matmul(scores[i][:], q_stack[:, s, i * P:(i + 1) * P], k_stack[:, s, :],
                                  start=True, stop=True).then_inc(scores_done, 1)

                def turn(n, j, i):
                    m = n * H + j
                    pe.wait_ge(exp_done, TPB + TPB * (m + 1))
                    pe.wait_ge((even_copied, odd_copied)[i % 2], 2 * m + i // 2)
                    for q in range(TPB):
                        last = pe.transpose(turned[i % 2][:, q, :], probs[:, j % 2, q, i * P:(i + 1) * P], g["ident"][:])
                    last.then_inc(probs_turned, 1)

                def weigh(n, j, i):
                    m = n * H + j
                    pe.wait_ge((even_copied, odd_copied)[i % 2], 2 * m + i // 2 + 1)
                    if i == 0:
                        pe.wait_ge(v_ready, m + 1)
                        if j == 0:
                            pe.wait_ge(out_copied, n)
                    last = pe.matmul(out_ps[:], v_head[:, j, i, :], probsT[:, j % 2, i, :],
                                     start=(j == 0 and i == 0), stop=(j == H - 1 and i == TPB - 1))
                    if i == TPB - 1:
                        last.then_inc(weighed, 1)

                def step(n, j, first, last):
                    before = (n, j - 1) if j else (n - 1, H - 1)
                    if first:
                        score(n, j)
                    if not last:
                        score(*((n, j + 1) if j + 1 < H else (n + 1, 0)))
                    for i in range(TPB):
                        turn(n, j, i)
                        if i % 2 == 1 and not first:
                            weigh(*before, i - 1)
                            weigh(*before, i)
                    if last:
                        for i in range(TPB):
                            weigh(n, j, i)

                steps(pe, step)

            @block.vector
            def _(dve):
                def maximum(n, j, i):
                    m = n * H + j
                    dve.wait_ge(scores_done, RING * TPB + TPB * m + i + 1)
                    dve.tensor_reduce(top[:, j % 2, i:i + 1], scores[i][:], AX, ALU.max, negate=True).then_inc(max_done, 1)

                def copy_out(n):
                    dve.wait_ge(weighed, H + (n + 1) * H)
                    dve.tensor_copy(out_flat[:, n, :], out_ps[:]).then_inc(out_copied, 1)

                def step(n, j, first, last):
                    m = n * H + j
                    if first:
                        for i in range(TPB):
                            maximum(n, j, i)
                    for i in range(TPB):
                        if not last:
                            maximum(*((n, j + 1) if j + 1 < H else (n + 1, 0)), i)
                        if i % 2 == 1:
                            dve.wait_ge(probs_turned, TPB * m + i + 1)
                            dve.tensor_copy(probsT[:, j % 2, i, :], turned[1][:].rearrange("p a b -> p (a b)")).then_inc(odd_copied, 1)
                    dve.tensor_copy(sums_flat[:, n, j, :], head_sums[:, j % 2, :]).then_inc(sums_copied, 1)
                    if j == 0 and not first:
                        copy_out(n - 1)
                    if last:
                        copy_out(n)

                steps(dve, step)

            @block.scalar
            def _(act):
                def exponent(n, j, i):
                    m = n * H + j
                    act.wait_ge(max_done, TPB * m + i + 1)
                    act.wait_ge(sums_copied, m + 1)
                    act.activation(probs[:, j % 2, i, :], scores[i][:], ACT.Exp, bias=top[:, j % 2, i:i + 1],
                                   accum_out=head_sums[:, j % 2, i:i + 1]).then_inc(exp_done, 1)

                def step(n, j, first, last):
                    m = n * H + j
                    if first:
                        for i in range(TPB):
                            exponent(n, j, i)
                    for i in range(TPB):
                        if i % 2 == 0:
                            act.wait_ge(probs_turned, TPB * m + i + 1)
                            act.activation(probsT[:, j % 2, i, :], turned[0][:].rearrange("p a b -> p (a b)"),
                                           ACT.Copy).then_inc(even_copied, 1)
                        if not last:
                            exponent(*((n, j + 1) if j + 1 < H else (n + 1, 0)), i)

                steps(act, step)


def project_attended(nc, g, attended, sums):
    with Scope(nc, "wout") as sc:
        wout = sc.sb("wout", [P, DT, D])
        shares = sc.sb("shares", [P, 2, TPB, P])
        weights = sc.sb("weights", [P, 2, DT, S])
        shares_ps = [sc.ps(f"shares{j}", [P, TPB, P]) for j in range(2)]
        out_ps = [sc.ps(f"out{j}", [P, D]) for j in range(2)]
        w_loaded = sc.sem("w_loaded")
        inverted = sc.sem("inverted")
        shares_ready = sc.sem("shares_ready")
        shares_turned = sc.sem("shares_turned")
        divided = sc.sem("divided")
        out_done = sc.sem("out_done")
        out_added = sc.sem("out_added")
        sums_flat = sums[:].rearrange("p b c h i -> p (b c) h i")
        with nc.Block() as block:
            @block.sync
            def _(sp):
                sp.sem_inc(shares_turned, 2)
                sp.sem_inc(divided, 2)
                sp.sem_inc(out_done, 2 * TPB)
                sp.sem_inc(out_added, 2)
                sp.dma_start(wout[:], g["wout"].rearrange("(k p) n -> p k n", p=P)).then_inc(w_loaded, 16)
                sp.wait_ge(w_loaded, 16)

            @block.scalar
            def _(act):
                act.wait_ge(inverted, 1)
                with act.Fori(0, B) as b:
                    for c in range(DT):
                        n = b * DT + c
                        act.wait_ge(shares_turned, n + 1)
                        for i in range(TPB):
                            last = act.activation(shares[:, c % 2, i, :].rearrange("p (h d) -> p h d", d=X_DIM),
                                                  sums_flat[:, n, :, i].unsqueeze(2).to_broadcast([P, HEADS_PER_TILE, X_DIM]), ACT.Copy)
                        last.then_inc(shares_ready, 1)

            @block.tensor
            def _(pe):
                pe.wait_ge(w_loaded, 16)
                with pe.Fori(0, B // 2) as bb:
                    for half in range(2):
                        for c in range(DT):
                            n = (2 * bb + half) * DT + c
                            pe.wait_ge(shares_ready, n + 1)
                            pe.wait_ge(divided, n + 1)
                            for i in range(TPB):
                                last = pe.transpose(shares_ps[c % 2][:, i, :], shares[:, c % 2, i, :], g["ident"][:])
                            last.then_inc(shares_turned, 1)
                    for half in range(2):
                        b = 2 * bb + half
                        pe.wait_ge(divided, 2 + DT * (b + 1))
                        for i in range(TPB):
                            pe.wait_ge(out_added, b * TPB + i + 1)
                            for c in range(DT):
                                last = pe.matmul(out_ps[i % 2][:], weights[:, half, c, i * P:(i + 1) * P], wout[:, c, :],
                                                 start=(c == 0), stop=(c == DT - 1))
                            last.then_inc(out_done, 1)

            @block.vector
            def _(dve):
                dve.reciprocal(sums_flat, sums_flat).then_inc(inverted, 1)
                with dve.Fori(0, B // 2) as bb:
                    for half in range(2):
                        b = 2 * bb + half
                        for c in range(DT):
                            dve.wait_ge(out_done, TPB * (b + 1))
                            dve.wait_ge(shares_turned, 2 + b * DT + c + 1)
                            dve.tensor_tensor(weights[:, half, c, :], attended[:, bass.ds(b, 1), c, :].rearrange("p o s -> p (o s)"),
                                              shares_ps[c % 2][:].rearrange("p a b -> p (a b)"), ALU.mult).then_inc(divided, 1)
                    for half in range(2):
                        for i in range(TPB):
                            t = (2 * bb + half) * TPB + i
                            dve.wait_ge(out_done, 2 * TPB + t + 1)
                            dve.tensor_tensor(g["x"][:, t, :], g["x"][:, t, :], out_ps[i % 2][:], ALU.add).then_inc(out_added, 1)



FFN = 1408
FT = FFN // P
FFN_CHUNKS = [(lo, min(S, FFN - lo)) for lo in range(0, FFN, S)]
FC = len(FFN_CHUNKS)
QFLOOR = 1e-5


def bitlinear_layer(nc, g):
    with Scope(nc, "ffn") as outer:
        h = outer.sb("h", [P, NT, D])
        wq = [outer.sb("w1q", [P, DT, FFN], BF16), outer.sb("w2q", [P, DT, FFN], BF16), outer.sb("w3q", [P, FT, D], BF16)]
        w_mean = outer.sb("w_mean", [P, 3])
        normalize_rows(nc, g, "ffn", h)

        with Scope(nc, "ternary") as sc:
            w = sc.sb("w", [P, 2, DT * FFN])
            clipped = sc.sb("clipped", [P, DT * FFN])
            part = sc.sb("part", [P, 3])
            inv = sc.sb("inv", [P, 3])
            total = [sc.ps(f"total{i}", [P, 1]) for i in range(3)]
            w_loaded = [sc.sem(f"w_loaded{i}") for i in range(3)]
            part_done = sc.sem("part_done")
            total_done = sc.sem("total_done")
            ternary_done = sc.sem("ternary_done")
            sources = [g["w1_T"], g["w2_T"], g["w3_T"]]
            with nc.Block() as block:
                @block.sync
                def _(sp):
                    for i in range(3):
                        n = sources[i].shape[1]
                        if i == 2:
                            sp.wait_ge(ternary_done, 1)
                        sp.dma_start(w[:, i % 2, :].rearrange("p (k n) -> p k n", n=n),
                                     sources[i].rearrange("(k p) n -> p k n", p=P)).then_inc(w_loaded[i], 16)
                    for i in range(3):
                        sp.wait_ge(w_loaded[i], 16)

                @block.vector
                def _(dve):
                    for i in range(3):
                        dve.wait_ge(w_loaded[i], 16)
                        dve.tensor_reduce(part[:, i:i + 1], w[:, i % 2, :], AX, ALU.add,
                                          apply_absolute_value=True).then_inc(part_done, 1)
                        dve.wait_ge(total_done, i + 1)
                        dve.tensor_scalar(w_mean[:, i:i + 1], total[i][:], 1.0 / (D * FFN), QFLOOR, ALU.mult, ALU.max)
                        dve.drain()
                        dve.reciprocal(inv[:, i:i + 1], w_mean[:, i:i + 1])
                        dve.drain()
                        dve.tensor_scalar(clipped[:], w[:, i % 2, :], inv[:, i:i + 1], -1.0, ALU.mult, ALU.max)
                        dve.drain()
                        dve.tensor_scalar(clipped[:], clipped[:], 1.0, ROUND, ALU.min, ALU.add)
                        dve.drain()
                        dve.tensor_scalar(wq[i][:].rearrange("p k n -> p (k n)"), clipped[:], ROUND, None,
                                          ALU.subtract).then_inc(ternary_done, 1)

                @block.tensor
                def _(pe):
                    for i in range(3):
                        pe.wait_ge(part_done, i + 1)
                        pe.matmul(total[i][:], g["ones"][:], part[:, i:i + 1], start=True, stop=True).then_inc(total_done, 1)

        with Scope(nc, "ternary_ffn") as sc:
            x_max = sc.sb("x_max", [P, 2])
            x_inv = sc.sb("x_inv", [P, 2])
            scales = sc.sb("scales", [P, 2, 3])
            rounded = sc.sb("rounded", [P, D])
            xq = sc.sb("xq", [P, D], BF16)
            xqT = sc.sb("xqT", [P, 2, DT, P], BF16)
            silu = sc.sb("silu", [P, 2, S])
            act_rows = sc.sb("act_rows", [P, FFN])
            act_rounded = sc.sb("act_rounded", [P, FFN])
            aq = sc.sb("aq", [P, FFN], BF16)
            aqT = sc.sb("aqT", [P, FT, P], BF16)
            xq_ps = sc.ps("xq_ps", [P, DT, P], BF16)
            gate_ps = [sc.ps(f"gate_ps{j}", [P, S]) for j in range(2)]
            up_ps = [sc.ps(f"up_ps{j}", [P, S]) for j in range(2)]
            aq_ps = sc.ps("aq_ps", [P, 2 * DT * 2, P], BF16)
            out_ps = sc.ps("out_ps", [P, D])
            xq_done = sc.sem("xq_done")
            xq_turned = sc.sem("xq_turned")
            xq_copied = sc.sem("xq_copied")
            hidden_done = sc.sem("hidden_done")
            silu_done = sc.sem("silu_done")
            act_done = sc.sem("act_done")
            aq_done = sc.sem("aq_done")
            aq_turned = sc.sem("aq_turned")
            aq_copied = sc.sem("aq_copied")
            out_done = sc.sem("out_done")
            out_added = sc.sem("out_added")

            def steps(engine, step):
                step(0, 0, True, False)
                with engine.Fori(0, (NT - 2) // 2) as pair:
                    for j in range(2):
                        step(2 * pair + 1 + j, (1 + j) % 2, False, False)
                step(NT - 1, (NT - 1) % 2, False, True)

            def buffer(p, c):
                return (p * FC + c) % 2

            with nc.Block() as block:
                @block.sync
                def _(sp):
                    sp.sem_inc(act_done, 2)
                    sp.sem_inc(out_added, 1)

                @block.vector
                def _(dve):
                    def quantize(t, p):
                        dve.tensor_reduce(x_max[:, 0:1], h[:, t, :], AX, ALU.max, apply_absolute_value=True)
                        dve.drain()
                        dve.tensor_scalar(x_max[:, 0:1], x_max[:, 0:1], QFLOOR, 1.0 / QMAX, ALU.max, ALU.mult)
                        dve.drain()
                        dve.reciprocal(x_inv[:, 0:1], x_max[:, 0:1])
                        dve.tensor_scalar(scales[:, p, 0:2], w_mean[:, 0:2], x_max[:, 0:1], None, ALU.mult)
                        dve.drain()
                        dve.tensor_scalar(rounded[:], h[:, t, :], x_inv[:, 0:1], ROUND, ALU.mult, ALU.add)
                        dve.drain()
                        dve.wait_ge(xq_turned, t)
                        dve.tensor_scalar(xq[:], rounded[:], ROUND, None, ALU.subtract).then_inc(xq_done, 1)

                    def activate(t, p):
                        for c, (lo, n) in enumerate(FFN_CHUNKS):
                            j = buffer(p, c)
                            dve.wait_ge(silu_done, t * FC + c + 1)
                            dve.scalar_tensor_tensor(act_rows[:, lo:lo + n], up_ps[j][:, 0:n], scales[:, p, 1:2],
                                                     silu[:, j, 0:n], ALU.mult, ALU.mult).then_inc(act_done, 1)
                        dve.drain()
                        dve.tensor_reduce(x_max[:, 1:2], act_rows[:], AX, ALU.max, apply_absolute_value=True)
                        dve.drain()
                        dve.tensor_scalar(x_max[:, 1:2], x_max[:, 1:2], QFLOOR, 1.0 / QMAX, ALU.max, ALU.mult)
                        dve.drain()
                        dve.reciprocal(x_inv[:, 1:2], x_max[:, 1:2])
                        dve.tensor_scalar(scales[:, p, 2:3], w_mean[:, 2:3], x_max[:, 1:2], None, ALU.mult)
                        dve.drain()
                        dve.tensor_scalar(act_rounded[:], act_rows[:], x_inv[:, 1:2], ROUND, ALU.mult, ALU.add)
                        dve.drain()
                        dve.wait_ge(aq_turned, t)
                        dve.tensor_scalar(aq[:], act_rounded[:], ROUND, None, ALU.subtract).then_inc(aq_done, 1)

                    def add(t, p):
                        dve.wait_ge(out_done, t + 1)
                        dve.scalar_tensor_tensor(g["x"][:, t, :], out_ps[:], scales[:, p, 2:3], g["x"][:, t, :],
                                                 ALU.mult, ALU.add).then_inc(out_added, 1)
                        dve.drain()

                    def step(t, p, first, last):
                        if first:
                            quantize(t, p)
                        if not last:
                            quantize(t + 1, 1 - p)
                        activate(t, p)
                        if not first:
                            add(t - 1, 1 - p)
                        if last:
                            add(t, p)

                    steps(dve, step)

                @block.tensor
                def _(pe):
                    def turn(t):
                        pe.wait_ge(xq_done, t + 1)
                        pe.wait_ge(xq_copied, t)
                        for k in range(DT):
                            last = pe.transpose(xq_ps[:, k, :], xq[:, k * P:(k + 1) * P], g["ident16"][:])
                        last.then_inc(xq_turned, 1)

                    def out(t):
                        pe.wait_ge(aq_copied, t + 1)
                        pe.wait_ge(out_added, t + 1)
                        for k in range(FT):
                            last = pe.matmul(out_ps[:], aqT[:, k, :], wq[2][:, k, :], start=(k == 0), stop=(k == FT - 1))
                        last.then_inc(out_done, 1)

                    def step(t, p, first, last_step):
                        if first:
                            turn(t)
                        pe.wait_ge(xq_copied, t + 1)
                        for c, (lo, n) in enumerate(FFN_CHUNKS):
                            pe.wait_ge(act_done, t * FC + c + 1)
                            for i, to in ((0, gate_ps), (1, up_ps)):
                                for k in range(DT):
                                    last = pe.matmul(to[buffer(p, c)][:, 0:n], xqT[:, p, k, :], wq[i][:, k, lo:lo + n],
                                                     start=(k == 0), stop=(k == DT - 1))
                            last.then_inc(hidden_done, 1)
                        if not last_step:
                            turn(t + 1)
                        if not first:
                            out(t - 1)
                        pe.wait_ge(aq_done, t + 1)
                        pe.wait_ge(aq_copied, t)
                        for k in range(FT):
                            last = pe.transpose(aq_ps[:, k, :], aq[:, k * P:(k + 1) * P], g["ident16"][:])
                        last.then_inc(aq_turned, 1)
                        if last_step:
                            out(t)

                    steps(pe, step)

                @block.scalar
                def _(act):
                    def copy(t, p):
                        act.wait_ge(xq_turned, t + 1)
                        act.activation(xqT[:, p, :, :], xq_ps[:], ACT.Copy).then_inc(xq_copied, 1)

                    def step(t, p, first, last):
                        if first:
                            copy(t, p)
                        for c, (lo, n) in enumerate(FFN_CHUNKS):
                            j = buffer(p, c)
                            act.wait_ge(hidden_done, t * FC + c + 1)
                            act.wait_ge(act_done, t * FC + c + 1)
                            act.activation(silu[:, j, 0:n], gate_ps[j][:, 0:n], ACT.Silu,
                                           scale=scales[:, p, 0:1]).then_inc(silu_done, 1)
                        if not last:
                            copy(t + 1, 1 - p)
                        act.wait_ge(aq_turned, t + 1)
                        act.wait_ge(out_done, t)
                        act.activation(aqT[:], aq_ps[:, 0:FT, :], ACT.Copy).then_inc(aq_copied, 1)

                    steps(act, step)



PHASES = [selective_scan_layer, smooth_quant_layer, expert_layer, delta_rule_layer, cross_attention_layer,
          bitlinear_layer]


def program(nc, arrays, phases):
    g = {name.removeprefix("in_"): nc.dram_tensor(name, a.shape, mybir.dt.from_np(a.dtype), kind="ExternalInput").ap()
         for name, a in arrays.items()}
    out = nc.dram_tensor("out_0_dram", (B, S, D), F32, kind="ExternalOutput").ap()
    g["out_dram"] = out.rearrange("b s d -> (b s) d")
    g["bc_dram"] = nc.dram_tensor("bc_dram", (2 * STATE, T), F32).ap()
    g["beta_dram"] = nc.dram_tensor("beta_dram", (HEADS, T), F32).ap()
    g["parts_dram"] = nc.dram_tensor("parts_dram", (2, PARTS, B, DT, P, S), BF16).ap()
    with Scope(nc, "main") as sc:
        g["x"] = sc.sb("x_rows", [P, NT, D])
        g["ident"] = sc.sb("ident", [P, P])
        g["ident16"] = sc.sb("ident16", [P, P], BF16)
        g["ones"] = sc.sb("ones", [P, P])
        load_constants(nc, g)
        for phase in phases:
            with nc.cleanup_on_exit():
                phase(nc, g)
        store_result(nc, g)


def lay_out(inputs):
    import numpy as np

    def turned(name):
        return np.ascontiguousarray(np.swapaxes(np.asarray(inputs[name]), -1, -2))

    def plain(name, *shape):
        return np.ascontiguousarray(np.asarray(inputs[name]).reshape(shape or np.shape(inputs[name])))

    def by_partition(name):
        return np.ascontiguousarray(np.asarray(inputs[name]).reshape(-1, P).T)

    def columns(name):
        return np.ascontiguousarray(np.moveaxis(np.asarray(inputs[name]).reshape(D, 2, HIDDEN), 1, 0))

    return {
        "in_x_dram": plain("x", T, D),
        "in_conv_w": plain("L0_attn_conv_w", D, TAPS),
        "in_conv_b": by_partition("L0_attn_conv_b"),
        "in_xproj_wT": turned("L0_attn_xproj_w"),
        "in_dtproj_wT": turned("L0_attn_dtproj_w"),
        "in_dt_b": by_partition("L0_attn_dtproj_b"),
        "in_a_log": plain("L0_attn_A_log"),
        "in_d_skip": by_partition("L0_attn_D_skip"),
        "in_gate_up_T": turned("fside_BxS2xS2_0"),
        "in_down_T": turned("ctx_1024"),
        "in_w_router": plain("L0_ffn_W_router"),
        "in_w_gate": np.concatenate([plain("L0_ffn_We_gate"), columns("L0_ffn_Ws_gate")]),
        "in_w_up": np.concatenate([plain("L0_ffn_We_up"), columns("L0_ffn_Ws_up")]),
        "in_w_down": np.concatenate([plain("L0_ffn_We_down"), plain("L0_ffn_Ws_down", 2, HIDDEN, D)]),
        "in_kda_wq": plain("L1_attn_Wq"),
        "in_kda_wk": plain("L1_attn_Wk"),
        "in_kda_wv": plain("L1_attn_Wv"),
        "in_conv_q_w": plain("L1_attn_conv_q_w"),
        "in_conv_q_b": by_partition("L1_attn_conv_q_b"),
        "in_conv_k_w": plain("L1_attn_conv_k_w"),
        "in_conv_k_b": by_partition("L1_attn_conv_k_b"),
        "in_conv_v_w": plain("L1_attn_conv_v_w"),
        "in_conv_v_b": by_partition("L1_attn_conv_v_b"),
        "in_kda_wfa": plain("L1_attn_Wfa"),
        "in_kda_wfb": plain("L1_attn_Wfb"),
        "in_kda_a_log": plain("L1_attn_A_log"),
        "in_dt_bias": by_partition("L1_attn_dt_bias"),
        "in_kda_wb": plain("L1_attn_Wb"),
        "in_kda_wga": plain("L1_attn_Wga"),
        "in_kda_wgb": plain("L1_attn_Wgb"),
        "in_o_norm_w": by_partition("L1_attn_o_norm_w"),
        "in_kda_wo": plain("L1_attn_Wo"),
        "in_ctx_T": turned("ctx_1024"),
        "in_pos": plain("fside_BxSx2_0", T, 2),
        "in_wq": plain("L1_xattn_Wq"),
        "in_wkv": plain("L1_xattn_Wkv"),
        "in_wout": plain("L1_xattn_Wout"),
        "in_bout": plain("L1_xattn_bout"),
        "in_w1_T": turned("L1_ffn_w1"),
        "in_w2_T": turned("L1_ffn_w2"),
        "in_w3_T": turned("L1_ffn_w3"),
    }


def kernel(**inputs):
    import concourse.bacc as _bacc
    from concourse.bass_utils import run_bass_kernel_spmd as _run

    nc = _bacc.Bacc("TRN2", target_bir_lowering=False, num_devices=1)
    arrays = lay_out(inputs)
    program(nc, arrays, PHASES)
    r = _run(nc, [arrays], core_ids=[0])
    return r.results[0]["out_0_dram"]
```
